# Optimizing a Trainium2 kernel written in Bass

```python
import numpy as np
import jax
import jax.numpy as jnp

def _softmax(x, axis=-1):
    return jax.nn.softmax(x, axis=axis)

def _gelu(x):
    return jax.nn.gelu(x, approximate=True)

def _silu(x):
    return jax.nn.silu(x)

def _sigmoid(x):
    return jax.nn.sigmoid(x)

def _layernorm(x, axis=-1, eps=1e-05):
    m = jnp.mean(x, axis=axis, keepdims=True)
    v = jnp.var(x, axis=axis, keepdims=True)
    return (x - m) / jnp.sqrt(v + eps)

def _scatter_add(tgt, idx, src, axis=0):
    return tgt.at[idx].add(src)

def _segment_sum(src, seg, n):
    return jax.ops.segment_sum(src, seg, n)
kernel_name = 'mk_macaron_d1_jaxref_r4_fd6251'

def setup_inputs(seed: int=0):
    np.random.seed(seed)
    _w = jnp.asarray

    def _L0_attn_setup():
        import jax, jax.numpy as jnp
        import numpy as np
        D_MODEL = 512
        N_HEADS = 16
        SEQ_LEN = 512
        BATCH = 2
        BIAS_MAX = 8.0

        def alibi_bias(n_heads, seq_len, dtype):
            pos = jnp.arange(1 - seq_len, 1, dtype=dtype)
            m = jnp.arange(1, n_heads + 1, dtype=dtype) * (BIAS_MAX / n_heads)
            slopes = 1.0 / 2.0 ** m
            return pos[None, :] * slopes[:, None]
        key = jax.random.key(seed)
        k1, k2, k3 = jax.random.split(key, 3)
        s = 1.0 / np.sqrt(D_MODEL)
        x = jax.random.normal(k1, (BATCH, SEQ_LEN, D_MODEL), dtype=jnp.float32)
        Wqkv = jax.random.normal(k2, (3 * D_MODEL, D_MODEL), dtype=jnp.float32) * s
        b_qkv = jnp.zeros((3 * D_MODEL,), dtype=jnp.float32)
        Wout = jax.random.normal(k3, (D_MODEL, D_MODEL), dtype=jnp.float32) * s
        b_out = jnp.zeros((D_MODEL,), dtype=jnp.float32)
        return {'x': x, 'Wqkv': Wqkv, 'b_qkv': b_qkv, 'Wout': Wout, 'b_out': b_out}
    _L0_attn_in = _L0_attn_setup()

    def _L0_ffn_setup():
        import jax, jax.numpy as jnp
        import numpy as np
        B, S, H, I, E, K = (4, 1024, 512, 256, 32, 4)
        key = jax.random.key(seed)
        k1, k2, k3, k4, k5, k6 = jax.random.split(key, 6)
        hidden_states = jax.random.normal(k1, (B, S, H), dtype=jnp.float32)
        topk_idx = jax.random.randint(k2, (B * S, K), 0, E)
        w = jax.random.uniform(k3, (B * S, K), dtype=jnp.float32)
        topk_weight = w / jnp.sum(w, axis=-1, keepdims=True)
        scale = 0.02
        gate_weight = jax.random.normal(k4, (E, I, H), dtype=jnp.float32) * scale
        up_weight = jax.random.normal(k5, (E, I, H), dtype=jnp.float32) * scale
        down_weight = jax.random.normal(k6, (E, H, I), dtype=jnp.float32) * scale
        return {'hidden_states': hidden_states, 'gate_weight': gate_weight, 'up_weight': up_weight, 'down_weight': down_weight, 'topk_idx': topk_idx, 'topk_weight': topk_weight}
    _L0_ffn_in = _L0_ffn_setup()
    _d = {'L0_attn_x': _L0_attn_in['x'], 'L0_attn_Wqkv': _L0_attn_in['Wqkv'], 'L0_attn_b_qkv': _L0_attn_in['b_qkv'], 'L0_attn_Wout': _L0_attn_in['Wout'], 'L0_attn_b_out': _L0_attn_in['b_out'], 'L0_ffn_gate_weight': _L0_ffn_in['gate_weight'], 'L0_ffn_up_weight': _L0_ffn_in['up_weight'], 'L0_ffn_down_weight': _L0_ffn_in['down_weight'], 'L0_ffn_topk_idx': _L0_ffn_in['topk_idx'], 'L0_ffn_topk_weight': _L0_ffn_in['topk_weight']}
    _x0 = _d['L0_attn_x']
    _d['L0_attn_x'] = jax.random.normal(jax.random.fold_in(jax.random.key(seed), 1), (8, 512, 512), dtype=_x0.dtype)
    del _x0
    return _d

def reference(L0_attn_x, L0_attn_Wqkv, L0_attn_b_qkv, L0_attn_Wout, L0_attn_b_out, L0_ffn_gate_weight, L0_ffn_up_weight, L0_ffn_down_weight, L0_ffn_topk_idx, L0_ffn_topk_weight):

    def _L0_attn_ref(x, Wqkv, b_qkv, Wout, b_out):
        import jax, jax.numpy as jnp
        import numpy as np
        D_MODEL = 512
        N_HEADS = 16
        SEQ_LEN = 512
        BATCH = 2
        BIAS_MAX = 8.0

        def alibi_bias(n_heads, seq_len, dtype):
            pos = jnp.arange(1 - seq_len, 1, dtype=dtype)
            m = jnp.arange(1, n_heads + 1, dtype=dtype) * (BIAS_MAX / n_heads)
            slopes = 1.0 / 2.0 ** m
            return pos[None, :] * slopes[:, None]
        B, S, D = x.shape
        H = N_HEADS
        hd = D // H
        scale = 1.0 / jnp.sqrt(jnp.asarray(hd, dtype=x.dtype))
        qkv = x @ Wqkv.T + b_qkv
        q, k, v = jnp.split(qkv, 3, axis=-1)
        q = q.reshape(B, S, H, hd)
        k = k.reshape(B, S, H, hd)
        v = v.reshape(B, S, H, hd)
        scores = jnp.einsum('bqhd,bkhd->bhqk', q, k) * scale
        bias = alibi_bias(H, S, x.dtype)
        scores = scores + bias[None, :, None, :]
        causal = jnp.tril(jnp.ones((S, S), dtype=bool))
        scores = jnp.where(causal[None, None, :, :], scores, jnp.asarray(-1000000000.0, dtype=x.dtype))
        p = jax.nn.softmax(scores, axis=-1)
        ctx = jnp.einsum('bhqk,bkhd->bqhd', p, v).reshape(B, S, D)
        return ctx @ Wout.T + b_out

    def _L0_ffn_ref(hidden_states, gate_weight, up_weight, down_weight, topk_idx, topk_weight):
        import jax, jax.numpy as jnp
        import numpy as np
        B, S, H, I, E, K = (4, 1024, 512, 256, 32, 4)
        b, s, h = hidden_states.shape
        n_experts = gate_weight.shape[0]
        top_k = topk_idx.shape[-1]
        x = hidden_states.reshape(-1, h)
        n = x.shape[0]
        flat_expert = topk_idx.reshape(-1)
        flat_weight = topk_weight.reshape(-1)
        perm = jnp.argsort(flat_expert)
        tok_sorted = jnp.repeat(jnp.arange(n), top_k)[perm]
        group_sizes = jnp.bincount(flat_expert, length=n_experts).astype(jnp.int32)
        xs = x[tok_sorted]
        g = jax.lax.ragged_dot(xs, jnp.swapaxes(gate_weight, 1, 2), group_sizes)
        u = jax.lax.ragged_dot(xs, jnp.swapaxes(up_weight, 1, 2), group_sizes)
        hmid = jax.nn.silu(g) * u
        o = jax.lax.ragged_dot(hmid, jnp.swapaxes(down_weight, 1, 2), group_sizes)
        o = o * flat_weight[perm][:, None]
        y = jnp.zeros((n, h), dtype=x.dtype).at[tok_sorted].add(o)
        return y.reshape(b, s, h)
    x = L0_attn_x
    x = x + 0.5 * _L0_ffn_ref(_layernorm(x, axis=-1), L0_ffn_gate_weight, L0_ffn_up_weight, L0_ffn_down_weight, L0_ffn_topk_idx, L0_ffn_topk_weight)
    x = x + _L0_attn_ref(_layernorm(x, axis=-1), L0_attn_Wqkv, L0_attn_b_qkv, L0_attn_Wout, L0_attn_b_out)
    x = x + 0.5 * _L0_ffn_ref(_layernorm(x, axis=-1), L0_ffn_gate_weight, L0_ffn_up_weight, L0_ffn_down_weight, L0_ffn_topk_idx, L0_ffn_topk_weight)
    return x

_drawn_inputs = setup_inputs


def setup_inputs(seed=0):
    import zlib

    import numpy as np

    out = dict(_drawn_inputs(seed))
    spreads = {'L0_attn_b_qkv': (0.0, 0.1), 'L0_attn_b_out': (0.0, 0.1)}
    factors = {'L0_ffn_gate_weight': 3.013,
     'L0_ffn_up_weight': 2.941,
     'L0_ffn_down_weight': 2.949,
     'L0_ffn_topk_weight': 6.257}
    for name, (base, spread) in spreads.items():
        noise = np.random.default_rng([zlib.crc32(name.encode()), seed]).standard_normal(out[name].shape)
        drawn = base * np.exp(spread * noise) if base else spread * noise
        out[name] = jnp.asarray(drawn.astype(out[name].dtype))
    for name, factor in factors.items():
        out[name] = (out[name] * factor).astype(out[name].dtype)
    return out
```

```python
from contextlib import ExitStack

import concourse.bass as bass
from concourse import mybir

P = 128
ALU = mybir.AluOpType
ACT = mybir.ActivationFunctionType
AX = mybir.AxisListType
F32 = mybir.dt.float32
F32R = mybir.dt.float32r
BF16 = mybir.dt.bfloat16
I32 = mybir.dt.int32

T, D, E, K, I = 4096, 512, 32, 4, 256
B, S, H, HD = 8, 512, 16, 32
NP = T * K
J = NP // P
NB = NP // P + E
NT = T // P
DC = D // P
IC = I // P
WROW = DC * 2 * I + IC * D
GU = DC * 2 * I
SLOT0 = 4
EPS = 1e-5
NEG = -1e30
FAR = 1 << 20
KROWS = 3 * HD + 4

C_ID, C_MQ, C_MK, C_TRI, C_ROW, C_COL, C_ONE = 0, P, 2 * P, 3 * P, 4 * P, 4 * P + 256, 4 * P + 257
C_END = C_ONE + P


def ds(start, size):
    return bass.ds(start, size)


def raw(ap):
    return ap.bitcast(F32)


class Chain:

    def __init__(self, eng, sem, base=0, per=0, turn=0):
        self.eng, self.sem, self.at, self.n = eng, sem, base + turn * per, 0

    def step(self, instruction):
        instruction.then_inc(self.sem, 1)
        self.n += 1
        self.eng.wait_ge(self.sem, self.at + self.n)


def below(b, n):
    return isinstance(b, int) and b < n


def moments(v, spare, st, k):
    v.sem_inc(spare, 1)
    return v.bn_aggr(st[:, k, 6:8], st[:, k, 0:6])


def inverse_deviation(g, spare, done, turn, st, rstd):
    g.sem_inc(spare, 1)
    g.tensor_scalar(rstd[:, 0, :], st[:, :, 7], EPS, None, ALU.add).then_inc(done, 1)
    g.wait_ge(done, turn * 2 + 1)
    g.tensor_tensor(rstd[:, 0, :], rstd[:, 0, :], rstd[:, 1, :], ALU.pow).then_inc(done, 1)


def route(nc, tb, const_d, idx_d, x_d, xn_d):
    with ExitStack() as c:
        sb = lambda name, shape, dt=F32: c.enter_context(nc.sbuf_tensor(f"r_{name}", shape, dt))
        sem = lambda name: c.enter_context(nc.semaphore(f"r_{name}"))
        CH = 8
        NCH = J // CH
        idx, idxf = sb("idx", [P, J], I32), sb("idxf", [P, J])
        onehot, cum = sb("onehot", [P, E, J]), sb("cum", [P, E, J])
        cnt = sb("cnt", [P, E])
        small = sb("small", [P, 6, E])
        prev, ends, nblk, first, last, off = (small[:, n, :] for n in range(6))
        nblk_i = sb("nblk_i", [P, E], I32)
        pos, posi, posf = sb("pos", [P, J]), sb("posi", [P, 2, J], I32), sb("posf", [P, 2, J])
        eqp = sb("eqp", [P, 2, CH, P], BF16)
        eqc = sb("eqc", [P, 2, CH, NB], BF16)
        val = sb("val", [P, 2, CH, 2, NB], BF16)
        pair = sb("pair", [P, 2, NB])
        ended = sb("ended", [1, NB + 2, E])
        bt = sb("bt", [1, 4, NB + 2])
        xt, xo = sb("xt", [P, 4, D]), sb("xo", [P, 4, D])
        st, rstd = sb("st", [P, 4, 8]), sb("rstd", [P, 2, 4])
        ps_cnt = c.enter_context(nc.psum_tensor("r_ps_cnt", [P, 2, E], F32))
        ps_pair = c.enter_context(nc.psum_tensor("r_ps_pair", [P, 2, NB], F32))
        s_in, s_v, s_cnt, s_pre = sem("in"), sem("v"), sem("cnt"), sem("pre")
        s_pos, s_eq, s_valp, s_valc = sem("pos"), sem("eq"), sem("valp"), sem("valc")
        s_mm, s_ln, s_spare, s_spare_g = sem("mm"), sem("ln"), sem("spare"), sem("spare_g")
        s_stat, s_mom, s_rstd = sem("stat"), sem("mom"), sem("rstd")
        s_x = [sem(f"x{k}") for k in range(4)]
        s_o = [sem(f"o{k}") for k in range(4)]
        cst = tb["cst"]

        def row(n):
            return cst[:, C_ROW:C_ROW + n]

        with nc.Block() as block:
            @block.sync
            def _(sp):
                sp.dma_start(cst[:, :], const_d).then_inc(s_in, 16)
                sp.dma_start(idx[:, :], idx_d).then_inc(s_in, 16)
                for k in range(4):
                    sp.dma_start(xt[:, k, :], x_d[k * P:(k + 1) * P, :]).then_inc(s_x[k], 16)
                with sp.Fori(0, NT // 4 - 1) as i:
                    for k in range(4):
                        sp.wait_ge(s_ln, i * 4 + (k + 1))
                        sp.dma_start(xn_d[ds((i * 4 + k) * P, P), :], xo[:, k, :]).then_inc(s_o[k], 16)
                        sp.dma_start(xt[:, k, :], x_d[ds((i * 4 + 4 + k) * P, P), :]).then_inc(s_x[k], 16)
                for k in range(4):
                    t = NT - 4 + k
                    sp.wait_ge(s_ln, t + 1)
                    sp.dma_start(xn_d[t * P:(t + 1) * P, :], xo[:, k, :]).then_inc(s_o[k], 16)
                for k in range(4):
                    sp.wait_ge(s_o[k], 16 * (NT // 4))

            @block.vector
            def _(v):
                ch = Chain(v, s_v)
                ch.step(v.memset(rstd[:, 1, :], -0.5))
                v.wait_ge(s_in, 32)
                ch.step(v.tensor_copy(idxf[:, :], idx[:, :]))
                ch.step(v.tensor_tensor(onehot[:, :, :], idxf[:, :].unsqueeze(1).to_broadcast([P, E, J]),
                                        row(E).unsqueeze(2).to_broadcast([P, E, J]), ALU.is_equal))
                flat = onehot[:, :, :].rearrange("p e j -> p (e j)")
                ch.step(v.tensor_tensor_scan(cum[:, :, :].rearrange("p e j -> p (e j)"), flat, flat,
                                             0.0, ALU.add, ALU.max))
                ch.step(v.memset(small[:, 0, 0:1], 0.0))
                ch.step(v.tensor_copy(ends, cum[:, :, J - 1]))
                ch.step(v.tensor_copy(small[:, 0, 1:E], small[:, 1, 0:E - 1]))
                v.tensor_tensor(cnt[:, :], ends, prev, ALU.subtract).then_inc(s_cnt, 1)
                v.wait_ge(s_pre, 1)
                ch.step(v.tensor_scalar(nblk, ps_cnt[:, 1, :], float(P - 1), None, ALU.add))
                ch.step(v.tensor_copy(nblk_i[:, :], nblk))
                ch.step(v.tensor_scalar(nblk_i[:, :], nblk_i[:, :], 7, None, ALU.arith_shift_right))
                ch.step(v.tensor_copy(nblk, nblk_i[:, :]))
                ch.step(v.tensor_tensor_scan(last, nblk, nblk, 0.0, ALU.add, ALU.max))
                ch.step(v.tensor_tensor(first, last, nblk, ALU.subtract))
                ch.step(v.tensor_scalar(first, first, float(P), -1.0, ALU.mult, ALU.add))
                ch.step(v.tensor_tensor(first, first, prev, ALU.subtract))
                ch.step(v.tensor_tensor(off, first, ps_cnt[:, 0, :], ALU.add))
                ch.step(v.tensor_tensor(cum[:, :, :], cum[:, :, :], off.unsqueeze(2).to_broadcast([P, E, J]),
                                        ALU.add))
                ch.step(v.tensor_tensor(cum[:, :, :], cum[:, :, :], onehot[:, :, :], ALU.mult))
                ch.step(v.tensor_reduce(pos[:, :], cum[:, :, :].rearrange("p e j -> p j e"), AX.X, ALU.add))
                ch.step(v.tensor_copy(posi[:, 0, :], pos[:, :]))
                ch.step(v.tensor_scalar(posi[:, 1, :], posi[:, 0, :], 7, None, ALU.arith_shift_right))
                ch.step(v.tensor_scalar(posi[:, 0, :], posi[:, 0, :], P - 1, None, ALU.bitwise_and))
                v.tensor_copy(posf[:, :, :], posi[:, :, :]).then_inc(s_pos, 1)
                v.wait_ge(s_pos, 1)
                with v.Fori(0, NCH // 2) as i:
                    for h in range(2):
                        q = i * 2 + h
                        v.wait_ge(s_mm, q + 1)
                        v.tensor_tensor(eqp[:, h, :, :],
                                        posf[:, 0, ds(q * CH, CH)].unsqueeze(2).to_broadcast([P, CH, P]),
                                        row(P).unsqueeze(1).to_broadcast([P, CH, P]), ALU.is_equal)
                        v.tensor_tensor(eqc[:, h, :, :],
                                        posf[:, 1, ds(q * CH, CH)].unsqueeze(2).to_broadcast([P, CH, NB]),
                                        row(NB).unsqueeze(1).to_broadcast([P, CH, NB]),
                                        ALU.is_equal).then_inc(s_eq, 1)
                with v.Fori(0, NT // 4) as i:
                    for k in range(4):
                        v.wait_ge(s_x[k], i * 16 + 16)
                        mom = v.bn_stats(st[:, k, 0:6], xt[:, k, :])
                    mom.then_inc(s_stat, 1)
                    v.wait_ge(s_stat, i + 1)
                    for k in range(4):
                        mom = moments(v, s_spare, st, k)
                    mom.then_inc(s_mom, 1)
                    v.wait_ge(s_rstd, i * 2 + 2)
                    for k in range(4):
                        v.wait_ge(s_o[k], i * 16)
                        v.tensor_scalar(xo[:, k, :], xt[:, k, :], st[:, k, 6:7], rstd[:, 0, k:k + 1],
                                        ALU.subtract, ALU.mult).then_inc(s_ln, 1)
                v.wait_ge(s_mm, NCH + 2)
                ch.step(v.tensor_scalar(pair[:, 0, :], ps_pair[:, 1, :], float(J), -1.0, ALU.mult, ALU.add))
                ch.step(v.tensor_scalar(pair[:, 1, :], ps_pair[:, 0, :], 0.0, float(FAR), ALU.is_equal, ALU.mult))
                ch.step(v.tensor_tensor(pair[:, 0, :], pair[:, 0, :], ps_pair[:, 0, :], ALU.add))
                ch.step(v.tensor_tensor(pair[:, 0, :], pair[:, 0, :], pair[:, 1, :], ALU.add))
                ch.step(v.tensor_copy(tb["pair"][:, :], pair[:, 0, :]))
                ch.step(v.tensor_scalar(tb["tok"][:, :], tb["pair"][:, :], 2, None, ALU.arith_shift_right))
                ch.step(v.tensor_tensor(ended[:, :, :], last[0:1, :].unsqueeze(1).to_broadcast([1, NB + 2, E]),
                                        cst[0:1, C_ROW:C_ROW + NB + 2].unsqueeze(2).to_broadcast([1, NB + 2, E]),
                                        ALU.is_le))
                ch.step(v.tensor_reduce(bt[:, 0, :], ended[:, :, :], AX.X, ALU.add))
                ch.step(v.tensor_scalar(bt[:, 0, :], bt[:, 0, :], float(E - 1), None, ALU.min))
                ch.step(v.memset(bt[:, 1, 0:1], 1.0))
                ch.step(v.tensor_tensor(bt[:, 1, 1:NB + 2], bt[:, 0, 1:NB + 2], bt[:, 0, 0:NB + 1],
                                        ALU.not_equal))
                ch.step(v.tensor_tensor_scan(bt[:, 2, :], bt[:, 1, :], bt[:, 1, :], 2.0, ALU.add, ALU.max))
                ch.step(v.tensor_scalar(bt[:, 3, :], bt[:, 2, :], 171.0, None, ALU.mult))
                ch.step(v.tensor_copy(tb["blk"][:, 2, :], bt[:, 3, :]))
                ch.step(v.tensor_scalar(tb["blk"][:, 2, :], tb["blk"][:, 2, :], 9, None, ALU.arith_shift_right))
                ch.step(v.tensor_copy(bt[:, 3, :], tb["blk"][:, 2, :]))
                ch.step(v.tensor_scalar(bt[:, 3, :], bt[:, 3, :], -3.0, None, ALU.mult))
                ch.step(v.tensor_tensor(bt[:, 3, :], bt[:, 3, :], bt[:, 2, :], ALU.add))
                ch.step(v.tensor_scalar(bt[:, 3, :], bt[:, 3, :], float(WROW), float(SLOT0), ALU.mult, ALU.add))
                ch.step(v.tensor_tensor(bt[:, 1, :], bt[:, 1, :], bt[:, 3, :], ALU.mult))
                ch.step(v.tensor_copy(tb["blk"][:, 0:2, :], bt[:, 0:2, :]))
                ch.step(v.tensor_copy(tb["blk"][:, 2, :], bt[:, 3, :]))

            @block.scalar
            def _(a):
                with a.Fori(0, NCH // 2) as i:
                    for h in range(2):
                        q = i * 2 + h
                        a.wait_ge(s_eq, q + 1)
                        a.activation(val[:, h, :, 1, :], eqc[:, h, :, :], ACT.Identity,
                                     scale=cst[:, C_COL:C_COL + 1]).then_inc(s_valp, 1)

            @block.gpsimd
            def _(g):
                with g.Fori(0, NCH // 2) as i:
                    for h in range(2):
                        q = i * 2 + h
                        g.wait_ge(s_eq, q + 1)
                        g.tensor_tensor(val[:, h, :, 0, :], eqc[:, h, :, :],
                                        cst[:, ds(q * CH + (C_ROW + 1), CH)].unsqueeze(2).to_broadcast([P, CH, NB]),
                                        ALU.mult).then_inc(s_valc, 1)
                with g.Fori(0, NT // 4) as i:
                    g.wait_ge(s_mom, i + 1)
                    inverse_deviation(g, s_spare_g, s_rstd, i, st, rstd)

            @block.tensor
            def _(pe):
                pe.sem_inc(s_mm, 2)
                pe.wait_ge(s_cnt, 1)
                pe.matmul(ps_cnt[:, 0, :], cst[:, C_TRI:C_TRI + P], cnt[:, :], start=True, stop=True)
                pe.matmul(ps_cnt[:, 1, :], cst[:, C_ONE:C_ONE + P], cnt[:, :], start=True,
                          stop=True).then_inc(s_pre, 1)

                def place(q, h, first, last):
                    pe.wait_ge(s_valp, q + 1)
                    pe.wait_ge(s_valc, q + 1)
                    for j in range(CH):
                        mm = pe.matmul(ps_pair[:, :, :].rearrange("p a n -> p (a n)"), eqp[:, h, j, :],
                                       val[:, h, j, :, :].rearrange("p a n -> p (a n)"),
                                       start=(first and j == 0), stop=(last and j == CH - 1),
                                       skip_group_check=True)
                    mm.then_inc(s_mm, 1)

                place(0, 0, True, False)
                place(1, 1, False, False)
                with pe.Fori(1, NCH // 2 - 1) as i:
                    for h in range(2):
                        place(i * 2 + h, h, False, False)
                place(NCH - 2, 0, False, False)
                place(NCH - 1, 1, False, True)


def moe(nc, tb, name, w_d, xn_d, y_d):
    with ExitStack() as c:
        sb = lambda n, shape, dt=F32: c.enter_context(nc.sbuf_tensor(f"{name}_{n}", shape, dt))
        ps = lambda n: c.enter_context(nc.psum_tensor(f"{name}_{n}", [P, 2, 512], F32))
        sem = lambda n: c.enter_context(nc.semaphore(f"{name}_{n}"))
        wraw = [sb(f"wraw{j}", [P, WROW]) for j in range(2)]
        wh, wl = sb("wh", [P, SLOT0 + 3 * WROW], F32R), sb("wl", [P, SLOT0 + 3 * WROW], F32R)
        it, ip = sb("it", [P, 2], I32), sb("ip", [P, 2], I32)
        xg = sb("xg", [P, 2, D])
        xh, xl = sb("xh", [P, 2, DC, P], F32R), sb("xl", [P, 2, DC, P], F32R)
        sg, hm = sb("sg", [P, 2, I]), sb("hm", [P, 2, I])
        hh, hl = sb("hh", [P, 2, IC, P], F32R), sb("hl", [P, 2, IC, P], F32R)
        ob = sb("ob", [P, 2, D])
        idle = sb("idle", [1, 2])
        psx, psg, psh, pso = ps("psx"), ps("psg"), ps("psh"), ps("pso")
        s_raw = [sem(f"raw{j}") for j in range(2)]
        s_gat = [sem(f"gat{j}") for j in range(2)]
        s_sca = [sem(f"sca{j}") for j in range(2)]
        s_wh, s_wl = sem("wh"), sem("wl")
        s_zero, s_it, s_ip, s_spare = sem("zero"), sem("it"), sem("ip"), sem("spare")
        s_spare_a, s_spare_v = sem("spare_a"), sem("spare_v")
        s_xt, s_xh, s_xl = sem("xt"), sem("xh"), sem("xl")
        s_gu, s_sg, s_hm = sem("gu"), sem("sg"), sem("hm")
        s_ht, s_hh, s_hl = sem("ht"), sem("hh"), sem("hl")
        s_dn, s_ob = sem("dn"), sem("ob")
        blk = tb["blk"]
        ident = tb["cst"][:, C_ID:C_ID + P]
        rounds = lambda b, j: (b - j) * 8

        def entry(eng, which, b):
            top = (E - 1, SLOT0 + 2 * WROW, SLOT0 + 2 * WROW)[which]
            return eng.value_load(blk[0:1, which, ds(b, 1)], min_val=0, max_val=top)

        with nc.Block() as block:
            @block.sync
            def _(sp):
                def load(b, j):
                    if not below(b, 2):
                        sp.wait_ge(s_wl, b - 1)
                    new, e = entry(sp, 1, b), entry(sp, 0, b)
                    with sp.If(new > 0):
                        sp.dma_start(wraw[j][:, :], w_d[ds(e * P, P), :]).then_inc(s_raw[j], 16)
                    with sp.Else():
                        sp.sem_inc(s_raw[j], 16)
                    sp.nop()

                load(0, 0)
                load(1, 1)
                with sp.Fori(1, NB // 2) as i:
                    for j in range(2):
                        load(i * 2 + j, j)

            @block.gpsimd
            def _(g):
                def gather(b, j):
                    if not below(b, 2):
                        g.wait_ge(s_xt, b - 1)
                    g.tensor_copy(it[:, j:j + 1], tb["tok"][:, ds(b, 1)]).then_inc(s_it, 1)
                    g.wait_ge(s_it, b + 1)
                    g.sem_inc(s_spare, 1)
                    g.indirect_dma_start(xg[:, j, :], None, xn_d, bass.IndirectOffsetOnAxis(it[:, j:j + 1], 0),
                                         bounds_check=tok_max, oob_is_err=False).then_inc(s_gat[j], 16)

                def scatter(b, j):
                    g.wait_ge(s_ob, b + 1)
                    g.tensor_copy(ip[:, j:j + 1], tb["pair"][:, ds(b, 1)]).then_inc(s_ip, 1)
                    g.wait_ge(s_ip, b + 1)
                    g.sem_inc(s_spare, 1)
                    g.indirect_dma_start(y_d, bass.IndirectOffsetOnAxis(ip[:, j:j + 1], 0), ob[:, j, :], None,
                                         bounds_check=pair_max, oob_is_err=False).then_inc(s_sca[j], 16)

                tok_max, pair_max = g.alloc_register(f"{name}_tok_max"), g.alloc_register(f"{name}_pair_max")
                g.reg_mov(tok_max, T - 1)
                g.reg_mov(pair_max, NP - 1)
                g.memset(idle[:, 0:1], 0.0)
                g.memset(xg[:, :, :], 0.0).then_inc(s_zero, 1)
                g.wait_ge(s_zero, 1)
                for b in range(4):
                    gather(b, b % 2)
                with g.Fori(2, NB // 2) as i:
                    for j in range(2):
                        gather(i * 2 + j, j)
                        scatter(i * 2 + (j - 4), j)
                for b in range(NB - 4, NB):
                    scatter(b, b % 2)
                for j in range(2):
                    g.wait_ge(s_sca[j], 16 * (NB // 2))

            @block.tensor
            def _(pe):
                def turn_x(b, j):
                    pe.wait_ge(s_gat[j], rounds(b, j) + 16)
                    if not below(b, 2):
                        pe.wait_ge(s_xl, b - 1)
                    for k in range(DC):
                        mm = pe.transpose(psx[:, j, k * P:(k + 1) * P], xg[:, j, k * P:(k + 1) * P], ident)
                    mm.then_inc(s_xt, 1)

                def gate_up(b, j):
                    at = pe.snap(slot[j], min_val=0, max_val=SLOT0 + 2 * WROW)
                    pe.wait_ge(s_wl, b + 1)
                    pe.wait_ge(s_xl, b + 1)
                    if not below(b, 2):
                        pe.wait_ge(s_hm, b - 1)
                    for k in range(DC):
                        cols = ds(at + k * 2 * I, 2 * I)
                        for n, (x, w) in enumerate(((xh, wh), (xh, wl), (xl, wh))):
                            mm = pe.matmul(psg[:, j, :], x[:, j, k, :], w[:, cols],
                                           start=(k == 0 and n == 0), stop=(k == DC - 1 and n == 2))
                    mm.then_inc(s_gu, 1)

                def down(b, j):
                    at = pe.snap(slot[j], min_val=0, max_val=SLOT0 + 2 * WROW)
                    pe.wait_ge(s_hl, b + 1)
                    if not below(b, 2):
                        pe.wait_ge(s_ob, b - 1)
                    for k in range(IC):
                        cols = ds(at + (GU + k * D), D)
                        for n, (h, w) in enumerate(((hh, wh), (hh, wl), (hl, wh))):
                            mm = pe.matmul(pso[:, j, :], h[:, j, k, :], w[:, cols],
                                           start=(k == 0 and n == 0), stop=(k == IC - 1 and n == 2))
                    mm.then_inc(s_dn, 1)

                def turn_h(b, j):
                    pe.wait_ge(s_hm, b + 1)
                    if not below(b, 2):
                        pe.wait_ge(s_hl, b - 1)
                    for k in range(IC):
                        mm = pe.transpose(psh[:, j, k * P:(k + 1) * P], hm[:, j, k * P:(k + 1) * P], ident)
                    mm.then_inc(s_ht, 1)

                slot = [pe.alloc_register(f"{name}_slot{j}") for j in range(2)]

                def find_slot(b, j):
                    pe.reg_load(slot[j], blk[0:1, 2, ds(b, 1)])

                def turn(b, j, last=False):
                    gate_up(b, j)
                    if not last:
                        turn_x(b + 1, 1 - j)
                    if not below(b, 1):
                        down(b - 1, 1 - j)
                    if not last:
                        find_slot(b + 1, 1 - j)
                    turn_h(b, j)

                turn_x(0, 0)
                find_slot(0, 0)
                turn(0, 0)
                turn(1, 1)
                with pe.Fori(1, NB // 2 - 1) as i:
                    for j in range(2):
                        turn(i * 2 + j, j)
                turn(NB - 2, 0)
                turn(NB - 1, 1, last=True)
                down(NB - 1, 1)

            @block.scalar
            def _(a):
                def weights_high(b, j, new):
                    a.wait_ge(s_raw[j], rounds(b, j) + 16)
                    if not below(b, 3):
                        a.wait_ge(s_dn, b - 2)
                    a.sem_inc(s_spare_a, 1)
                    with a.If(new > 0):
                        a.activation(wh[:, ds(new, WROW)], wraw[j][:, :], ACT.Copy).then_inc(s_wh, 1)
                    with a.Else():
                        a.activation(idle[:, 0:1], idle[:, 0:1], ACT.Copy).then_inc(s_wh, 1)
                    a.nop()

                def rows_high(b, j):
                    a.wait_ge(s_xt, b + 1)
                    if not below(b, 2):
                        a.wait_ge(s_gu, b - 1)
                    a.activation(xh[:, j, :, :], psx[:, j, :].rearrange("p (k n) -> p k n", k=DC),
                                 ACT.Copy).then_inc(s_xh, 1)

                def silu(b, j):
                    a.wait_ge(s_gu, b + 1)
                    if not below(b, 2):
                        a.wait_ge(s_hm, b - 1)
                    a.activation(sg[:, j, :], psg[:, j, 0:I], ACT.Silu).then_inc(s_sg, 1)

                def result(b, j):
                    a.wait_ge(s_dn, b + 1)
                    if not below(b, 2):
                        a.wait_ge(s_sca[j], rounds(b, j))
                    a.activation(ob[:, j, :], pso[:, j, :], ACT.Copy).then_inc(s_ob, 1)

                def product_high(b, j):
                    a.wait_ge(s_ht, b + 1)
                    if not below(b, 2):
                        a.wait_ge(s_dn, b - 1)
                    a.activation(hh[:, j, :, :], psh[:, j, 0:I].rearrange("p (k n) -> p k n", k=IC),
                                 ACT.Copy).then_inc(s_hh, 1)

                def turn(b, j, ahead=True):
                    new = entry(a, 1, b + 2) if ahead else None
                    silu(b, j)
                    if not isinstance(b, int) or b + 1 < NB:
                        rows_high(b + 1, 1 - j)
                    if not below(b, 1):
                        result(b - 1, 1 - j)
                    product_high(b, j)
                    if ahead:
                        weights_high(b + 2, j, new)

                a.wait_ge(s_zero, 1)
                weights_high(0, 0, entry(a, 1, 0))
                weights_high(1, 1, entry(a, 1, 1))
                rows_high(0, 0)
                turn(0, 0)
                turn(1, 1)
                with a.Fori(1, NB // 2 - 1) as i:
                    for j in range(2):
                        turn(i * 2 + j, j)
                turn(NB - 2, 0, ahead=False)
                turn(NB - 1, 1, ahead=False)
                result(NB - 1, 1)

            @block.vector
            def _(v):
                def weights_low(b, j, new):
                    v.wait_ge(s_wh, b + 1)
                    v.sem_inc(s_spare_v, 1)
                    with v.If(new > 0):
                        v.tensor_tensor(wl[:, ds(new, WROW)], wraw[j][:, :], wh[:, ds(new, WROW)].bitcast(F32),
                                        ALU.subtract).then_inc(s_wl, 1)
                    with v.Else():
                        v.memset(idle[:, 1:2], 0.0).then_inc(s_wl, 1)
                    v.nop()

                def rows_low(b, j):
                    v.wait_ge(s_xh, b + 1)
                    v.tensor_tensor(xl[:, j, :, :], psx[:, j, :].rearrange("p (k n) -> p k n", k=DC),
                                    xh[:, j, :, :].bitcast(F32), ALU.subtract).then_inc(s_xl, 1)

                def product(b, j):
                    v.wait_ge(s_sg, b + 1)
                    if not below(b, 2):
                        v.wait_ge(s_ht, b - 1)
                    v.tensor_tensor(hm[:, j, :], sg[:, j, :], psg[:, j, I:2 * I], ALU.mult).then_inc(s_hm, 1)

                def product_low(b, j):
                    v.wait_ge(s_hh, b + 1)
                    v.tensor_tensor(hl[:, j, :, :], psh[:, j, 0:I].rearrange("p (k n) -> p k n", k=IC),
                                    hh[:, j, :, :].bitcast(F32), ALU.subtract).then_inc(s_hl, 1)

                def turn(b, j, ahead=True):
                    new = entry(v, 1, b + 2) if ahead else None
                    product(b, j)
                    if not isinstance(b, int) or b + 1 < NB:
                        rows_low(b + 1, 1 - j)
                    product_low(b, j)
                    if ahead:
                        weights_low(b + 2, j, new)

                weights_low(0, 0, entry(v, 1, 0))
                weights_low(1, 1, entry(v, 1, 1))
                rows_low(0, 0)
                turn(0, 0)
                turn(1, 1)
                with v.Fori(1, NB // 2 - 1) as i:
                    for j in range(2):
                        turn(i * 2 + j, j)
                turn(NB - 2, 0, ahead=False)
                turn(NB - 1, 1, ahead=False)


def attend(nc, tb, d):
    NG, HG, TB = H // 4, 4, S // P
    CQ = 3 * D
    STK = 16 * (2 * HG + 2)
    SCALE = float(HD) ** -0.5
    RY, NY = 4, TB * K

    def uses(last):
        found = []
        for g in range(NG):
            if not (last and g >= 2):
                found += [("q", g), ("k", g)]
            if g == 1 and not last:
                found += [("x", t) for t in range(TB)]
            if g == 3 and not last:
                found += [("v", t) for t in range(TB)]
            if not (last and g == 3):
                found += [("m", g)]
            if g == 3:
                found += [("o", t) for t in range(TB)]
        return found

    FIRST = [("x", t) for t in range(TB)] + [("q", 0), ("k", 0), ("q", 1), ("k", 1), ("m", 0)]
    FIRST += [("v", t) for t in range(TB)]
    N0, NU = len(FIRST), len(uses(False))
    A0 = AU = TB
    D0, DU = N0 - A0, NU - AU

    class Bank:

        def __init__(self, b):
            self.b = b
            self.first = b is None
            self.order = FIRST if self.first else uses(isinstance(b, int))
            self.base = 0 if self.first else b * NU + N0

        def number(self, name, i):
            return self.base + self.order.index((name, i))

        def bank(self, name, i):
            return (self.order.index((name, i)) + (0 if self.first else N0)) % 2

        def reads(self, n):
            acts = sum(x == "v" for x, _ in self.order[:max(n, 0)])
            vecs = max(n, 0) - acts
            if self.first:
                return acts, vecs
            if n < 0:
                vecs -= 1
            return self.b * AU + (A0 + acts), self.b * DU + (D0 + vecs)

        def freed(self, name, i):
            return self.reads(self.order.index((name, i)) - 1)

        def read(self, name, i):
            return self.reads(self.order.index((name, i)) + 1)

    with ExitStack() as c:
        sb = lambda n, shape, dt=F32: c.enter_context(nc.sbuf_tensor(f"a_{n}", shape, dt))
        ps = lambda n, shape: c.enter_context(nc.psum_tensor(f"a_{n}", shape, F32))
        sem = lambda n: c.enter_context(nc.semaphore(f"a_{n}"))
        cst = tb["cst"]
        ident = cst[:, C_ID:C_ID + P]
        wqkv = [sb(f"wqkv_{n}", [P, DC, CQ], F32R) for n in "hl"]
        wout = [sb(f"wout_{n}", [P, DC, D], F32R) for n in "hl"]
        bqk = sb("bqk", [P, 2 * DC])
        wk = sb("wk", [P, NT * K])
        masks = sb("masks", [P, 3, P], BF16)
        stq, stk = sb("stq", [KROWS, 2 * HG, S], F32R), sb("stk", [KROWS, 2 * HG, S], F32R)
        qk3 = sb("qk3", [P, 2, 3, S], F32R)
        biases = sb("biases", [34, 2, S], F32R)
        bias_r, brow = biases[0:H, :, :], biases[32:34, :, :]
        y4 = sb("y4", [P, RY, D])
        xt = sb("xt", [P, TB, D])
        xn = sb("xn", [P, 2, D])
        free = sb("free", [P, 1])
        xth, xtl = sb("xth", [P, DC, S], F32R), sb("xtl", [P, DC, S], F32R)
        vt = sb("vt", [P, TB, D])
        mx = sb("mx", [P, 2, HG * TB])
        mh, ml = sb("mh", [HG * TB, P], F32R), sb("ml", [34, P], F32R)
        ones2 = ml[32:34, :]
        ml = ml[0:HG * TB, :]
        pt = [sb("pt0", [P, HG, S]), sb("pt1", [P, HG, S - P])]
        ct = sb("ct", [P, S])
        cth, ctl = sb("cth", [P, DC, S], F32R), sb("ctl", [P, DC, S], F32R)
        x2 = sb("x2", [P, TB, D])
        st, rstd = sb("st", [P, 2, 4, 8]), sb("rstd", [P, 2, 2, 4])
        s_spare_v, s_spare_g, s_spare_s = sem("spare_v"), sem("spare_g"), sem("spare_s")

        with ExitStack() as c1:
            bias, ones_r = xt[0:H, 0, :], qk3[0:H, 0, 0, :]
            rows, rows_l, ones = xt[32:33, 1:3, :], xth[32:33, 0:2, :], xt[32:34, 0, 0:P]
            sem1 = lambda n: c1.enter_context(nc.semaphore(f"a_{n}"))
            s_wh, s_wl, s_rows, s_in, s_c, s_bh, s_bl = (sem1(n) for n in ("wh", "wl", "rows", "in", "c", "bh", "bl"))
            s_ld = [sem1(f"ld{r}") for r in range(RY)]
            pieces = [(k, n) for n in range(4) for k in range(DC)]
            half = lambda w, k, n: wqkv[w][:, k, n * D:(n + 1) * D] if n < 3 else wout[w][:, k, :]
            with nc.Block() as block:
                @block.sync
                def _(sp):
                    for i, (k, n) in enumerate(pieces):
                        if i >= RY:
                            sp.wait_ge(s_wl, i - RY + 1)
                        sp.dma_start(y4[:, i % RY, :], d["wqkv"][:, k, n * D:(n + 1) * D] if n < 3
                                     else d["wout"][:, k, :]).then_inc(s_ld[i % RY], 16)
                    sp.wait_ge(s_c, 2)
                    for row in (0, 1):
                        for st_, at in ((stq, 3 * HD), (stk, 3 * HD + 2)):
                            sp.dma_start(raw(st_[at + row:at + row + 1, :, :]),
                                         raw(qk3[0:2 * HG, 0, 0, :])).then_inc(s_rows, 16)
                    sp.wait_ge(s_bl, 1)
                    sp.dma_start(raw(biases[33:34, :, :]), raw(rows_l)).then_inc(s_rows, 16)
                    sp.wait_ge(s_rows, 80)

                @block.scalar
                def _(a):
                    for dst, src in ((bqk[:, :], d["bqk"]), (rows, d["bvo"]), (wk[:, :], d["wk"]),
                                     (bias, d["bias"])):
                        a.dma_start(dst, src).then_inc(s_in, 16)
                    for i, (k, n) in enumerate(pieces):
                        a.wait_ge(s_ld[i % RY], 16 * (i // RY + 1))
                        a.activation(half(0, k, n), y4[:, i % RY, :], ACT.Copy,
                                     scale=1.0 if n else SCALE).then_inc(s_wh, 1)
                    a.wait_ge(s_in, 64)
                    a.activation(bqk[:, 0:DC], bqk[:, 0:DC], ACT.Copy, scale=SCALE)
                    a.activation(biases[32:33, :, :], rows, ACT.Copy).then_inc(s_bh, 1)

                @block.vector
                def _(v):
                    for i, (k, n) in enumerate(pieces):
                        v.wait_ge(s_wh, i + 1)
                        v.scalar_tensor_tensor(half(1, k, n), y4[:, i % RY, :], 1.0 if n else SCALE,
                                               half(0, k, n).bitcast(F32), ALU.mult,
                                               ALU.subtract).then_inc(s_wl, 1)
                    v.wait_ge(s_bh, 1)
                    v.tensor_tensor(rows_l, rows, biases[32:33, :, :].bitcast(F32), ALU.subtract).then_inc(s_bl, 1)

                @block.gpsimd
                def _(g):
                    g.memset(ones, 1.0)
                    g.memset(bias_r[:, 1, :].bitcast(F32), 1.0).then_inc(s_c, 1)
                    g.wait_ge(s_c, 1)
                    g.tensor_copy(ones2, ones)
                    g.tensor_copy(ones_r, bias_r[:, 1, :].bitcast(F32)).then_inc(s_c, 1)
                    g.wait_ge(s_c, 2)
                    g.wait_ge(s_in, 64)
                    g.tensor_copy(bias_r[:, 0, :], bias).then_inc(s_c, 1)
                    g.wait_ge(s_c, 3)
                    g.tensor_tensor(bias_r[:, 1, :], bias, bias_r[:, 0, :].bitcast(F32), ALU.subtract)
                    g.tensor_copy(masks[:, :, :], cst[:, C_ID:C_ID + 3 * P].rearrange("p (m n) -> p m n", m=3))
                    g.tensor_scalar(wk[:, :], wk[:, :], 0.5, None, ALU.mult)
                    g.memset(rstd[:, :, 1, :], -0.5)

        psa, psb, psw = ps("psa", [P, 2, S]), ps("psb", [P, 2, S]), ps("psw", [P, 2, S])
        psc, pss = ps("psc", [P, S]), ps("pss", [P, S])
        s_y = [sem(f"y{r}") for r in range(RY)]
        s_xin, s_acc, s_x1o = sem("xin"), sem("acc"), sem("x1o")
        s_st, s_mom, s_rd, s_xn = sem("st"), sem("mom"), sem("rd"), sem("xn")
        s_w, s_wfa, s_wfd = sem("w"), sem("wfa"), sem("wfd")
        s_xh, s_qc, s_qh, s_stk = sem("xh"), sem("qc"), sem("qh"), sem("stk")
        s_a, s_am, s_mh, s_mr = sem("a"), sem("am"), sem("mh"), sem("mr")
        s_b, s_e, s_pv = sem("b"), sem("e"), sem("pv")
        s_rs, s_ct, s_cc, s_ch = sem("rs"), sem("ct"), sem("cc"), sem("ch")
        s_xr, s_x2, s_x2o = sem("xr"), sem("x2"), sem("x2o")
        s_mom2, s_rd2, s_n2, s_n2o = sem("mom2"), sem("rd2"), sem("n2"), sem("n2o")
        whole = lambda b: isinstance(b, int)

        with nc.Block() as block:
            @block.sync
            def _(sp):
                def load_x(b):
                    if not (whole(b) and b == 0):
                        sp.wait_ge(s_xn, b * TB)
                        sp.sem_inc(s_spare_s, 1)
                        sp.wait_ge(s_x1o, b * 16)
                        sp.sem_inc(s_spare_s, 1)
                        sp.wait_ge(s_n2o, b * 16 - 16)
                    sp.sem_inc(s_spare_s, 1)
                    sp.dma_start(xt[:, :, :], d["x"][ds(b * S, S), :].rearrange("(t p) n -> p t n", p=P)
                                 ).then_inc(s_xin, 16)

                def load_rows(b, some):
                    for m in some:
                        k, t, r = m // TB, m % TB, m % RY
                        if not (whole(b) and b == 0 and m < RY):
                            sp.wait_ge(s_acc, b * NY + (m - RY + 1))
                        sp.sem_inc(s_spare_s, 1)
                        sp.dma_start(y4[:, r, :], d["y"][ds((b * S + t * P) * K, P * K), :].rearrange(
                            "(p k) n -> p k n", k=K)[:, k, :]).then_inc(s_y[r], 16)

                def store_x1(b):
                    sp.wait_ge(s_acc, b * NY + NY)
                    sp.sem_inc(s_spare_s, 1)
                    sp.dma_start(d["x1"][ds(b * S, S), :].rearrange("(t p) n -> p t n", p=P), xt[:, :, :]
                                 ).then_inc(s_x1o, 16)

                def stacks(u, g4):
                    slot = (g4 % 2) * HG
                    sp.wait_ge(s_qh, u + 1)
                    if not below(u, 2):
                        sp.wait_ge(s_b, u * 16 - 16)
                    for j in range(HG):
                        rows = slice(j * HD, (j + 1) * HD)
                        for n, to in enumerate((stq, stk)):
                            sp.dma_start(raw(to[0:3 * HD, slot + j, :]), raw(qk3[rows, n, :, :])).then_inc(s_stk, 16)
                    for r in range(2):
                        sp.dma_start(raw(stk[3 * HD + r:3 * HD + r + 1, slot:slot + HG, :]),
                                     raw(bias_r[g4 * HG:(g4 + 1) * HG, r, :])).then_inc(s_stk, 16)

                def outputs(b):
                    at = ds(b * S, S)
                    sp.wait_ge(s_x2, b + 1)
                    sp.sem_inc(s_spare_s, 1)
                    sp.dma_start(d["x2"][at, :].rearrange("(t p) n -> p t n", p=P), x2[:, :, :]).then_inc(s_x2o, 16)
                    sp.wait_ge(s_n2, b + 1)
                    sp.sem_inc(s_spare_s, 1)
                    sp.dma_start(d["xn"][at, :].rearrange("(t p) n -> p t n", p=P), xt[:, :, :]).then_inc(s_n2o, 16)

                def residual(b):
                    if not (whole(b) and b == 0):
                        sp.wait_ge(s_x2o, b * 16)
                        sp.sem_inc(s_spare_s, 1)
                        sp.wait_ge(s_n2, b)
                        sp.sem_inc(s_spare_s, 1)
                    sp.wait_ge(s_x1o, b * 16 + 16)
                    sp.sem_inc(s_spare_s, 1)
                    sp.dma_start(x2[:, :, :], d["x1"][ds(b * S, S), :].rearrange("(t p) n -> p t n", p=P)
                                 ).then_inc(s_xr, 16)

                def batch(b):
                    last = whole(b)
                    for g in range(NG):
                        if g == 0 and not last:
                            load_rows(b + 1, range(RY))
                            load_x(b + 1)
                            load_rows(b + 1, range(RY, NY // 2))
                        if g == 1 and not last:
                            load_rows(b + 1, range(NY // 2 + RY, NY))
                        if not (last and g >= 2):
                            stacks(b * NG + (g + 2), (g + 2) % NG)
                        if g == 0 and not last:
                            load_rows(b + 1, range(NY // 2, NY // 2 + RY))
                        if g == 1 and not last:
                            store_x1(b + 1)
                        if g == 1:
                            residual(b)
                    outputs(b)

                load_x(0)
                load_rows(0, range(NY))
                store_x1(0)
                stacks(0, 0)
                stacks(1, 1)
                with sp.Fori(0, B - 1) as b:
                    batch(b)
                batch(B - 1)
                sp.wait_ge(s_x2o, 16 * B)
                sp.wait_ge(s_n2o, 16 * B)

            @block.gpsimd
            def _(g):
                def inverse(b, which, mom, rd):
                    g.wait_ge(mom, b + 1)
                    inverse_deviation(g, s_spare_g, rd, b, st[:, which, :, :], rstd[:, which, :, :])

                def split_context(b, g4):
                    u = b * NG + g4
                    g.wait_ge(s_ct, u + 1)
                    g.wait_ge(s_w, b * NU + N0)
                    g.sem_inc(s_spare_g, 1)
                    g.tensor_copy(cth[:, g4, :], ct[:, :]).then_inc(s_cc, 1)
                    g.wait_ge(s_cc, u + 1)
                    g.tensor_tensor(ctl[:, g4, :], ct[:, :], cth[:, g4, :].bitcast(F32),
                                    ALU.subtract).then_inc(s_ch, 1)

                def batch(b):
                    last = whole(b)
                    for g4 in range(NG):
                        if g4 == 1 and not last:
                            inverse(b + 1, 0, s_mom, s_rd)
                        split_context(b, g4)
                    inverse(b, 1, s_mom2, s_rd2)

                inverse(0, 0, s_mom, s_rd)
                with g.Fori(0, B - 1) as b:
                    batch(b)
                batch(B - 1)

            @block.tensor
            def _(pe):
                def take(bk, name, i):
                    acts, vecs = bk.freed(name, i)
                    for s, n in ((s_wfa, acts), (s_wfd, vecs)):
                        if not (bk.first and n == 0):
                            pe.wait_ge(s, n)
                    return psw[:, bk.bank(name, i), :]

                def product(out, lhs, rhs, chunks, begun=False):
                    for k in chunks:
                        for n, (p, q) in enumerate(((0, 0), (0, 1), (1, 0))):
                            mm = pe.matmul(out, lhs[p](k), rhs[q](k), start=(k == 0 and n == 0 and not begun),
                                           stop=(k == DC - 1 and n == 2))
                    return mm

                def biased(out, which, lhs, rhs):
                    pe.matmul(out, ones2, brow[:, which, :], start=True, stop=False)
                    return product(out, lhs, rhs, range(DC), begun=True)

                def turn_x(bk, nb, t):
                    out = take(bk, "x", t)
                    pe.wait_ge(s_xn, nb * TB + (t + 1))
                    for k in range(DC):
                        mm = pe.transpose(out[:, k * P:(k + 1) * P], xn[:, t % 2, k * P:(k + 1) * P], ident)
                    mm.then_inc(s_w, 1)

                def project(out, g4, n, chunks):
                    cols = slice(n * D + g4 * P, n * D + (g4 + 1) * P)
                    return product(out, [lambda k, w=w: w[:, k, cols] for w in wqkv],
                                   [lambda k, x=x: x[:, k, :] for x in (xth, xtl)], chunks)

                def scores_row(u, slot, j):
                    h = slot * HG + j
                    for t in range(TB):
                        n = j * TB + t
                        if not (below(u, 1) and n < 2):
                            pe.wait_ge(s_am, u * 16 + (n - 1))
                        out = psa[:, t % 2, 0:(t + 1) * P]
                        pe.matmul(out, stq[0:3 * HD + 2, h, t * P:(t + 1) * P], stk[0:3 * HD + 2, h, 0:(t + 1) * P],
                                  start=True, stop=False)
                        pe.matmul(psa[:, t % 2, t * P:(t + 1) * P], masks[:, 0, :], masks[:, 1, :],
                                  start=False, stop=True).then_inc(s_a, 1)

                def turn_maxima(bk, u, i, slot):
                    out = take(bk, "m", i)
                    pe.wait_ge(s_am, u * 16 + 16)
                    pe.transpose(out[0:HG * TB, 0:P], mx[:, slot, :], ident).then_inc(s_w, 1)

                def values(bk, tiles):
                    for t in tiles:
                        out = take(bk, "v", t)
                        biased(out, 0, [lambda k, x=x: x[:, k, t * P:(t + 1) * P] for x in (xth, xtl)],
                               [lambda k, w=w: w[:, k, 2 * D:3 * D] for w in wqkv]).then_inc(s_w, 1)

                def output(bk, b):
                    pe.wait_ge(s_ch, b * NG + NG)
                    for t in range(TB):
                        out = take(bk, "o", t)
                        biased(out, 1, [lambda k, x=x: x[:, k, t * P:(t + 1) * P] for x in (cth, ctl)],
                               [lambda k, w=w: w[:, k, :] for w in wout]).then_inc(s_w, 1)

                def context(u, g, kt, part):
                    if part == 0:
                        pe.wait_ge(s_e, u * 16 + (kt * HG + HG + 1))
                        if kt == 0 and not below(u, 1):
                            pe.wait_ge(s_ct, u)
                    for j in range(HG):
                        at = (g * HG + j) * HD
                        mm = pe.matmul((psc, pss)[part][j * HD:(j + 1) * HD, kt * P:S],
                                       cst[:, C_ONE:C_ONE + HD] if part else vt[:, kt, at:at + HD],
                                       pt[kt % 2][:, j, 0:S - kt * P], start=(kt == 0), stop=(kt == TB - 1),
                                       skip_group_check=True)
                    if part == 1:
                        mm.then_inc(s_pv, 1)

                def attention(bk, b, g, qk_on):
                    u = b * NG + g
                    pe.wait_ge(s_mr, u * 32 + 32)
                    if g == 0:
                        pe.wait_ge(s_wfa, b * TB + TB)
                    for kt in range(TB):
                        for j in range(HG):
                            n, h = kt * HG + j, (g % 2) * HG + j
                            pe.wait_ge(s_e, u * 16 + n)
                            out = psb[:, n % 2, 0:S - kt * P]
                            pe.matmul(out, stk[:, h, kt * P:(kt + 1) * P], stq[:, h, kt * P:S],
                                      start=True, stop=False)
                            pe.matmul(psb[:, n % 2, 0:P], masks[:, 0, :], masks[:, 2, :],
                                      start=False, stop=True).then_inc(s_b, 1)
                            if kt == 0 and qk_on:
                                if j == 0:
                                    k_out = take(bk, "k", g)
                                mm = project(k_out, (g + 2) % NG, 1, (j,))
                                if j == HG - 1:
                                    mm.then_inc(s_w, 1)
                            if kt and j % 2:
                                context(u, g, kt - 1, j // 2)
                    for part in (0, 1):
                        context(u, g, TB - 1, part)

                def batch(b):
                    last, bk = whole(b), Bank(b)
                    for g in range(NG):
                        u = b * NG + g
                        qk_on, a_on = not (last and g >= 2), not (last and g == 3)
                        if qk_on:
                            out = take(bk, "q", g)
                            if g == 2:
                                pe.wait_ge(s_wfd, bk.read("x", TB - 1)[1])
                            project(out, (g + 2) % NG, 0, range(DC)).then_inc(s_w, 1)
                        attention(bk, b, g, qk_on)
                        if a_on:
                            pe.wait_ge(s_stk, u * STK + 2 * STK)
                            if g == 3:
                                values(bk, (0, 1))
                            for j in range(HG):
                                scores_row(u + 1, (g + 1) % 2, j)
                                if g == 1 and j and not last:
                                    turn_x(bk, b + 1, j - 1)
                                if g == 3 and j < 2:
                                    values(bk, (2 + j,))
                            if g == 1 and not last:
                                turn_x(bk, b + 1, TB - 1)
                            turn_maxima(bk, u + 1, g, (g + 1) % 2)
                    output(bk, b)

                bk = Bank(None)
                pe.sem_inc(s_pv, 1)
                for t in range(TB):
                    turn_x(bk, 0, t)
                pe.wait_ge(s_wfd, TB)
                for g in range(2):
                    for n, name in enumerate("qk"):
                        project(take(bk, name, g), g, n, range(DC)).then_inc(s_w, 1)
                pe.wait_ge(s_stk, STK)
                for j in range(HG):
                    scores_row(0, 0, j)
                turn_maxima(bk, 0, 0, 0)
                values(bk, range(TB))
                with pe.Fori(0, B - 1) as b:
                    batch(b)
                batch(B - 1)

            @block.scalar
            def _(a):
                def high(bk, u, i, g4, n):
                    name = "qk"[n]
                    a.wait_ge(s_w, bk.number(name, i) + 1)
                    if not below(u, 1):
                        a.wait_ge(s_stk, u * STK)
                    a.activation(qk3[:, n, 0:2 + n:1 + n, :],
                                 psw[:, bk.bank(name, i), :].unsqueeze(1).to_broadcast([P, 2, S]), ACT.Identity,
                                 bias=bqk[:, n * DC + g4:n * DC + g4 + 1]).then_inc(s_qc, 1)

                def rows_high(bk, b):
                    for t in range(TB):
                        a.wait_ge(s_w, bk.number("x", t) + 1)
                        a.activation(xth[:, :, t * P:(t + 1) * P],
                                     psw[:, bk.bank("x", t), :].rearrange("p (k n) -> p k n", k=DC),
                                     ACT.Copy).then_inc(s_xh, 1)

                def values(bk):
                    for t in range(TB):
                        a.wait_ge(s_w, bk.number("v", t) + 1)
                        a.activation(vt[:, t, :], psw[:, bk.bank("v", t), :], ACT.Copy).then_inc(s_wfa, 1)

                def probabilities(u, kt):
                    for j in range(HG):
                        n = kt * HG + j
                        a.wait_ge(s_b, u * 16 + (n + 1))
                        if j == 0:
                            a.wait_ge(s_pv, u * 4 + kt)
                        a.activation(pt[kt % 2][:, j, 0:S - kt * P], psb[:, n % 2, 0:S - kt * P],
                                     ACT.Exp).then_inc(s_e, 1)

                def maxima(u, slot):
                    a.wait_ge(s_mh, u * 2 + 2)
                    for r, m in enumerate((mh, ml)):
                        at = 3 * HD + 2 + r
                        a.dma_start(raw(stq[at:at + 1, slot * HG:(slot + 1) * HG, :].rearrange(
                            "a h (t q) -> a (h t) q", q=P)), raw(m[:, :])).then_inc(s_mr, 16)

                def batch(b):
                    last, bk = whole(b), Bank(b)
                    for g in range(NG):
                        u = b * NG + g
                        for kt in range(TB):
                            if kt in (0, 2) and not (last and g >= 2):
                                high(bk, u + 2, g, (g + 2) % NG, kt // 2)
                            probabilities(u, kt)
                        if g == 1 and not last:
                            rows_high(bk, b + 1)
                        if g == 3 and not last:
                            values(bk)
                        if not (last and g == 3):
                            maxima(u + 1, (g + 1) % 2)

                bk = Bank(None)
                a.sem_inc(s_e, 1)
                rows_high(bk, 0)
                for u in range(2):
                    for n in range(2):
                        high(bk, u, u, u, n)
                maxima(0, 0)
                values(bk)
                with a.Fori(0, B - 1) as b:
                    batch(b)
                batch(B - 1)

            @block.vector
            def _(v):
                def sums(b, some):
                    for m in some:
                        k, t, r = m // TB, m % TB, m % RY
                        if m == 0:
                            v.wait_ge(s_xin, b * 16 + 16)
                        v.wait_ge(s_y[r], b * (NY // RY * 16) + (m // RY + 1) * 16)
                        if k:
                            v.wait_ge(s_acc, b * NY + (m - TB + 1))
                        v.scalar_tensor_tensor(xt[:, t, :], y4[:, r, :], wk[:, ds(b * NY + (t * K + k), 1)],
                                               xt[:, t, :], ALU.mult, ALU.add).then_inc(s_acc, 1)

                def means(b):
                    v.wait_ge(s_acc, b * NY + NY)
                    for t in range(TB):
                        ins = v.bn_stats(st[:, 0, t, 0:6], xt[:, t, :])
                    ins.then_inc(s_st, 1)
                    v.wait_ge(s_st, b + 1)
                    for t in range(TB):
                        ins = moments(v, s_spare_v, st[:, 0, :, :], t)
                    ins.then_inc(s_mom, 1)

                def normed(out, src, which, t):
                    return v.tensor_scalar(out, src, st[:, which, t, 6:7], rstd[:, which, 0, t:t + 1],
                                           ALU.subtract, ALU.mult)

                def row(bk, b, t):
                    if t == 0:
                        v.wait_ge(s_rd, b * 2 + 2)
                    if t >= 2:
                        v.wait_ge(s_w, bk.number("x", t - 2) + 1)
                    normed(xn[:, t % 2, :], xt[:, t, :], 0, t).then_inc(s_xn, 1)

                def row_low(bk, b, t):
                    v.wait_ge(s_xh, b * TB + (t + 1))
                    at = slice(t * P, (t + 1) * P)
                    v.tensor_tensor(xtl[:, :, at], psw[:, bk.bank("x", t), :].rearrange("p (k n) -> p k n", k=DC),
                                    xth[:, :, at].bitcast(F32), ALU.subtract).then_inc(s_wfd, 1)

                def low(bk, u, i, g4, n):
                    v.wait_ge(s_qc, u * 2 + (n + 1))
                    v.scalar_tensor_tensor(qk3[:, n, 2 - n, :], psw[:, bk.bank("qk"[n], i), :],
                                           bqk[:, n * DC + g4:n * DC + g4 + 1], qk3[:, n, 0, :].bitcast(F32),
                                           ALU.add, ALU.subtract).then_inc(s_wfd, 1)
                    if n:
                        v.memset(free[:, :], 0.0).then_inc(s_qh, 1)

                def maxima(u, slot, j):
                    for t in range(TB):
                        n = j * TB + t
                        v.wait_ge(s_a, u * 16 + (n + 1))
                        v.tensor_reduce(mx[:, slot, n:n + 1], psa[:, t % 2, 0:(t + 1) * P], AX.X,
                                        ALU.max).then_inc(s_am, 1)

                def negated(bk, u, i):
                    src = psw[0:HG * TB, bk.bank("m", i), 0:P]
                    v.wait_ge(s_w, bk.number("m", i) + 1)
                    if not below(u, 1):
                        v.wait_ge(s_mr, u * 32)
                    v.tensor_scalar(mh[:, :], src, -1.0, None, ALU.mult).then_inc(s_mh, 1)
                    v.wait_ge(s_mh, u * 2 + 1)
                    v.scalar_tensor_tensor(ml[:, :], src, -1.0, mh[:, :].bitcast(F32), ALU.mult,
                                           ALU.subtract).then_inc(s_mh, 1)
                    v.wait_ge(s_mh, u * 2 + 2)
                    v.memset(free[:, :], 0.0).then_inc(s_wfd, 1)

                def normalise(u):
                    v.wait_ge(s_pv, u * 4 + 5)
                    if not below(u, 1):
                        v.wait_ge(s_ch, u)
                    v.reciprocal(ct[:, :], pss[:, :]).then_inc(s_rs, 1)
                    v.wait_ge(s_rs, u + 1)
                    v.tensor_tensor(ct[:, :], psc[:, :], ct[:, :], ALU.mult).then_inc(s_ct, 1)

                def output(bk, b):
                    v.wait_ge(s_xr, b * 16 + 16)
                    for t in range(TB + 1):
                        if t < TB:
                            v.wait_ge(s_w, bk.number("o", t) + 1)
                            v.tensor_tensor(x2[:, t, :], psw[:, bk.bank("o", t), :], x2[:, t, :],
                                            ALU.add).then_inc(s_wfd, 1)
                        if t:
                            v.wait_ge(s_wfd, bk.read("o", t - 1)[1])
                            ins = v.bn_stats(st[:, 1, t - 1, 0:6], x2[:, t - 1, :])
                    ins.then_inc(s_x2, 1)
                    v.wait_ge(s_x2, b + 1)
                    for t in range(TB):
                        ins = moments(v, s_spare_v, st[:, 1, :, :], t)
                    ins.then_inc(s_mom2, 1)
                    if whole(b):
                        v.wait_ge(s_n2o, (B - 1) * 16)
                    else:
                        v.wait_ge(s_x1o, b * 16 + 32)
                    v.wait_ge(s_rd2, b * 2 + 2)
                    for t in range(TB):
                        ins = normed(xt[:, t, :], x2[:, t, :], 1, t)
                    ins.then_inc(s_n2, 1)

                def batch(b):
                    last, bk = whole(b), Bank(b)
                    for g in range(NG):
                        u = b * NG + g
                        for n in range(2):
                            if not (last and g >= 2):
                                low(bk, u + 2, g, (g + 2) % NG, n)
                            if g < 2 and not last:
                                at = (2 * g + n) * RY
                                sums(b + 1, range(at, at + RY))
                        if g == 1 and not last:
                            means(b + 1)
                        if g == 3:
                            normalise(u)
                        if not (last and g == 3):
                            for j in range(HG):
                                maxima(u + 1, (g + 1) % 2, j)
                                if g == 1 and not last:
                                    if j >= 2:
                                        row_low(bk, b + 1, j - 2)
                                    row(bk, b + 1, j)
                            if g == 1 and not last:
                                for t in (2, 3):
                                    row_low(bk, b + 1, t)
                            negated(bk, u + 1, g)
                        if g < 3:
                            normalise(u)
                    output(bk, b)

                bk = Bank(None)
                sums(0, range(NY))
                means(0)
                for t in range(TB + 2):
                    if t >= 2:
                        row_low(bk, 0, t - 2)
                    if t < TB:
                        row(bk, 0, t)
                for u in range(2):
                    for n in range(2):
                        low(bk, u, u, u, n)
                for j in range(HG):
                    maxima(0, 0, j)
                negated(bk, 0, 0)
                with v.Fori(0, B - 1) as b:
                    batch(b)
                batch(B - 1)


def final(nc, tb, d, out_d):
    with ExitStack() as c:
        sb = lambda n, shape, dt=F32: c.enter_context(nc.sbuf_tensor(f"z_{n}", shape, dt))
        sem = lambda n: c.enter_context(nc.semaphore(f"z_{n}"))
        R = 4
        y4, xt = sb("y4", [P, R, K, D]), sb("xt", [P, R, D])
        wk = sb("wk", [P, NT * K])
        s_w, s_w2 = sem("w"), sem("w2")
        s_in = [sem(f"in{r}") for r in range(R)]
        s_out = [sem(f"out{r}") for r in range(R)]
        s_done = [sem(f"done{r}") for r in range(R)]
        s_acc_v, s_acc_g, s_scaled, s_spare_s = sem("acc_v"), sem("acc_g"), sem("scaled"), sem("spare_s")
        with nc.Block() as block:
            @block.sync
            def _(sp):
                sp.dma_start(wk[:, :], d["wk"]).then_inc(s_w, 16)

                def load(i, r):
                    t = i * R + r
                    sp.dma_start(y4[:, r, :, :], d["y"][ds(t * (P * K), P * K), :].rearrange(
                        "(p k) n -> p k n", k=K)).then_inc(s_in[r], 16)
                    sp.dma_start(xt[:, r, :], d["x2"][ds(t * P, P), :]).then_inc(s_in[r], 16)

                def store(i, r):
                    sp.wait_ge(s_done[r], i + 1)
                    sp.sem_inc(s_spare_s, 1)
                    sp.dma_start(out_d[ds((i * R + r) * P, P), :], xt[:, r, :]).then_inc(s_out[r], 16)

                for r in range(R):
                    load(0, r)
                with sp.Fori(0, NT // R - 1) as i:
                    for r in range(R):
                        store(i, r)
                        sp.wait_ge(s_out[r], i * 16 + 16)
                        sp.sem_inc(s_spare_s, 1)
                        load(i + 1, r)
                for r in range(R):
                    store(NT // R - 1, r)
                for r in range(R):
                    sp.wait_ge(s_out[r], NT // R * 16)

            @block.vector
            def _(v):
                v.wait_ge(s_w, 16)
                v.tensor_scalar(wk[:, :], wk[:, :], 0.5, None, ALU.mult).then_inc(s_w2, 1)
                v.wait_ge(s_w2, 1)
                with v.Fori(0, NT // R) as i:
                    for m, r in enumerate(range(0, R, 2)):
                        t, at = i * R + r, i * (R // 2 * (K - 1)) + m * (K - 1)
                        v.wait_ge(s_in[r], i * 32 + 32)
                        for k in range(K):
                            if k:
                                v.wait_ge(s_acc_v, at + k)
                            v.scalar_tensor_tensor(xt[:, r, :], y4[:, r, k, :], wk[:, ds(t * K + k, 1)],
                                                   xt[:, r, :], ALU.mult, ALU.add).then_inc(
                                                       s_acc_v if k < K - 1 else s_done[r], 1)

            @block.scalar
            def _(a):
                a.wait_ge(s_w2, 1)
                with a.Fori(0, NT // R) as i:
                    for r in range(1, R, 2):
                        t = i * R + r
                        a.wait_ge(s_in[r], i * 32 + 32)
                        for k in range(K):
                            ins = a.activation(y4[:, r, k, :], y4[:, r, k, :], ACT.Copy,
                                               scale=wk[:, ds(t * K + k, 1)])
                        ins.then_inc(s_scaled, 1)

            @block.gpsimd
            def _(g):
                with g.Fori(0, NT // R) as i:
                    for m, r in enumerate(range(1, R, 2)):
                        at = i * (R // 2 * (K - 1)) + m * (K - 1)
                        g.wait_ge(s_scaled, i * (R // 2) + (m + 1))
                        for k in range(K):
                            if k:
                                g.wait_ge(s_acc_g, at + k)
                            g.tensor_tensor(xt[:, r, :], xt[:, r, :], y4[:, r, k, :], ALU.add).then_inc(
                                s_acc_g if k < K - 1 else s_done[r], 1)


def macaron(nc, x, idx, wk, w, wqkv, bqk, bvo, wout, const, bias, out):
    with ExitStack() as c:
        sb = lambda n, shape, dt=F32: c.enter_context(nc.sbuf_tensor(n, shape, dt))
        tb = {"cst": sb("cst", [P, C_END]),
              "pair": sb("pair", [P, NB], I32),
              "tok": sb("tok", [P, NB], I32),
              "blk": sb("blk", [1, 3, NB + 2], I32)}
        hbm = lambda n, shape: nc.dram_tensor(n, shape, F32, kind="Internal").ap()
        xn = hbm("xn_rows", (T, D))
        y = hbm("y_rows", (NP, D))
        d = {"x": x, "y": y, "wk": wk, "wqkv": wqkv, "bqk": bqk, "bvo": bvo, "wout": wout,
             "bias": bias, "x1": hbm("x1_rows", (T, D)), "x2": hbm("x2_rows", (T, D)), "xn": xn}
        route(nc, tb, const, idx, x, xn)
        moe(nc, tb, "f1", w, xn, y)
        attend(nc, tb, d)
        moe(nc, tb, "f2", w, xn, y)
        final(nc, tb, d, out)




def constants():
    import numpy as np
    c, r = np.zeros((P, C_END), np.float32), np.arange(P)
    c[:, C_ID:C_ID + P] = np.eye(P)
    c[:, C_MQ:C_MQ + P] = np.where(r[None, :] > r[:, None], NEG, 0.0)
    c[:, C_MK:C_MK + P] = np.where(r[:, None] > r[None, :], NEG, 0.0)
    c[:, C_TRI:C_TRI + P] = r[:, None] < r[None, :]
    c[:, C_ROW:C_ROW + 256] = np.arange(256)
    c[:, C_COL] = r
    c[:, C_ONE:C_ONE + P] = 1.0
    return c


def alibi():
    import numpy as np
    m = np.arange(1, H + 1, dtype=np.float32) * np.float32(8.0 / H)
    slopes = (np.float32(1.0) / np.float32(2.0) ** m).astype(np.float32)
    return (np.arange(1 - S, 1, dtype=np.float32)[None, :] * slopes[:, None]).astype(np.float32)


def kernel(L0_attn_x, L0_attn_Wqkv, L0_attn_b_qkv, L0_attn_Wout, L0_attn_b_out, L0_ffn_gate_weight,
           L0_ffn_up_weight, L0_ffn_down_weight, L0_ffn_topk_idx, L0_ffn_topk_weight):
    import numpy as np
    import concourse.bacc as bacc
    from concourse.bass_utils import run_bass_kernel_spmd

    put = lambda a: np.ascontiguousarray(a)
    turned = lambda a, n: np.asarray(a).transpose(0, 2, 1).reshape(E, n, P, -1)
    gu = np.concatenate([turned(L0_ffn_gate_weight, DC), turned(L0_ffn_up_weight, DC)], -1)
    gu = gu.transpose(0, 2, 1, 3).reshape(E, P, GU)
    dn = turned(L0_ffn_down_weight, IC).transpose(0, 2, 1, 3).reshape(E, P, IC * D)
    chunked = lambda a: np.asarray(a).T.reshape(DC, P, -1).transpose(1, 0, 2)
    b_qkv = np.asarray(L0_attn_b_qkv)
    arrays = {
        "x_in": put(np.asarray(L0_attn_x).reshape(T, D)),
        "idx_in": put(np.asarray(L0_ffn_topk_idx).reshape(P, J)),
        "wk_in": put(np.asarray(L0_ffn_topk_weight).reshape(NT, P, K).transpose(1, 0, 2).reshape(P, NT * K)),
        "w_in": put(np.concatenate([gu, dn], -1).reshape(E * P, WROW)),
        "wqkv_in": put(chunked(L0_attn_Wqkv)),
        "bqk_in": put(b_qkv[:2 * D].reshape(2 * DC, P).T),
        "bvo_in": put(np.stack([b_qkv[2 * D:], np.asarray(L0_attn_b_out)])[None]),
        "wout_in": put(chunked(L0_attn_Wout)),
        "const_in": constants(),
        "bias_in": alibi(),
    }
    nc = bacc.Bacc("TRN2", target_bir_lowering=False, num_devices=1)
    args = [nc.dram_tensor(n, a.shape, mybir.dt.from_np(a.dtype), kind="ExternalInput").ap()
            for n, a in arrays.items()]
    out = nc.dram_tensor("out", (T, D), F32, kind="ExternalOutput").ap()
    macaron(nc, *args, out)
    r = run_bass_kernel_spmd(nc, [arrays], core_ids=[0])
    return r.results[0]["out"].reshape(B, S, D)
```

```python
from contextlib import ExitStack

import concourse.bass as bass
from concourse import mybir

P = 128
ALU = mybir.AluOpType
ACT = mybir.ActivationFunctionType
AX = mybir.AxisListType
F32 = mybir.dt.float32
F32R = mybir.dt.float32r
BF16 = mybir.dt.bfloat16
I32 = mybir.dt.int32

T, D, E, K, I = 4096, 512, 32, 4, 256
B, S, H, HD = 8, 512, 16, 32
NP = T * K
J = NP // P
NB = NP // P + E
NT = T // P
DC = D // P
IC = I // P
WROW = DC * 2 * I + IC * D
GU = DC * 2 * I
NS = 4
SLOT0 = 4
EPS = 1e-5
NEG = -1e30
FAR = 1 << 20
KROWS = 3 * HD + 4

C_ID, C_MQ, C_MK, C_ONE, C_KEEP = 0, P, 2 * P, 3 * P, 4 * P
C_TRI, C_ROW, C_COL, C_END = C_KEEP, C_KEEP + P, C_KEEP + P + 256, C_KEEP + P + 257


def ds(start, size):
    return bass.ds(start, size)


def raw(ap):
    return ap.bitcast(F32)


class Chain:

    def __init__(self, eng, sem, base=0, per=0, turn=0):
        self.eng, self.sem, self.at, self.n = eng, sem, base + turn * per, 0

    def step(self, instruction):
        instruction.then_inc(self.sem, 1)
        self.n += 1
        self.eng.wait_ge(self.sem, self.at + self.n)


def below(b, n):
    return isinstance(b, int) and b < n


def moments(v, spare, st, k):
    v.sem_inc(spare, 1)
    return v.bn_aggr(st[:, k, 6:8], st[:, k, 0:6])


def inverse_deviation(g, spare, done, turn, st, rstd):
    g.sem_inc(spare, 1)
    g.tensor_scalar(rstd[:, 0, :], st[:, :, 7], EPS, None, ALU.add).then_inc(done, 1)
    g.wait_ge(done, turn * 2 + 1)
    g.tensor_tensor(rstd[:, 0, :], rstd[:, 0, :], rstd[:, 1, :], ALU.pow).then_inc(done, 1)


def route(nc, tb, const_d, idx_d, x_d, xn_d):
    with ExitStack() as c:
        sb = lambda name, shape, dt=F32: c.enter_context(nc.sbuf_tensor(f"r_{name}", shape, dt))
        sem = lambda name: c.enter_context(nc.semaphore(f"r_{name}"))
        CH = 8
        NCH = J // CH
        assert NCH == NT // 2
        idx, idxf = sb("idx", [P, J], I32), sb("idxf", [P, J])
        onehot, cum = sb("onehot", [P, E, J]), sb("cum", [P, E, J])
        cnt = sb("cnt", [P, E])
        small = sb("small", [P, 6, E])
        prev, ends, nblk, first, last, off = (small[:, n, :] for n in range(6))
        nblk_i = sb("nblk_i", [P, E], I32)
        pos, posi, posf = sb("pos", [P, J]), sb("posi", [P, 2, J], I32), sb("posf", [P, 2, J])
        eqp = sb("eqp", [P, 2, CH, P], BF16)
        eqc = sb("eqc", [P, 2, CH, NB], BF16)
        val = sb("val", [P, 2, CH, 2, NB], BF16)
        pair = sb("pair", [P, 2, NB])
        ended = sb("ended", [1, NB + 2, E])
        bt = sb("bt", [1, 4, NB + 2])
        xt, xo = sb("xt", [P, 4, D]), sb("xo", [P, 4, D])
        st, rstd = sb("st", [P, 4, 8]), sb("rstd", [P, 2, 4])
        ps_cnt = c.enter_context(nc.psum_tensor("r_ps_cnt", [P, 2, E], F32))
        ps_pair = c.enter_context(nc.psum_tensor("r_ps_pair", [P, 2, NB], F32))
        s_in, s_v, s_cnt, s_pre = sem("in"), sem("v"), sem("cnt"), sem("pre")
        s_pos, s_eq, s_valp, s_valc = sem("pos"), sem("eq"), sem("valp"), sem("valc")
        s_mm, s_ln, s_spare, s_spare_g = sem("mm"), sem("ln"), sem("spare"), sem("spare_g")
        s_stat, s_mom, s_rstd = sem("stat"), sem("mom"), sem("rstd")
        s_x = [sem(f"x{k}") for k in range(4)]
        s_o = [sem(f"o{k}") for k in range(4)]
        cst, cst_r = tb["cst"], sb("cst", [P, C_END - C_KEEP])

        def routing(column, n):
            return cst_r[:, ds(column - C_KEEP, n)]

        def row(n):
            return routing(C_ROW, n)

        with nc.Block() as block:
            @block.sync
            def _(sp):
                sp.dma_start(cst[:, :], const_d[:, 0:C_KEEP]).then_inc(s_in, 16)
                sp.dma_start(cst_r[:, :], const_d[:, C_KEEP:C_END]).then_inc(s_in, 16)
                sp.dma_start(idx[:, :], idx_d).then_inc(s_in, 16)
                for k in range(4):
                    sp.dma_start(xt[:, k, :], x_d[k * P:(k + 1) * P, :]).then_inc(s_x[k], 16)
                    sp.sem_inc(s_o[k], 16)
                with sp.Fori(0, NT // 4 - 1) as i:
                    for k in range(4):
                        sp.wait_ge(s_ln, i * 4 + (k + 1))
                        sp.dma_start(xn_d[ds((i * 4 + k) * P, P), :], xo[:, k, :]).then_inc(s_o[k], 16)
                        sp.dma_start(xt[:, k, :], x_d[ds((i * 4 + 4 + k) * P, P), :]).then_inc(s_x[k], 16)
                for k in range(4):
                    t = NT - 4 + k
                    sp.wait_ge(s_ln, t + 1)
                    sp.dma_start(xn_d[t * P:(t + 1) * P, :], xo[:, k, :]).then_inc(s_o[k], 16)
                for k in range(4):
                    sp.wait_ge(s_o[k], 16 * (NT // 4) + 16)

            @block.vector
            def _(v):
                ch = Chain(v, s_v)
                ch.step(v.memset(rstd[:, 1, :], -0.5))
                v.wait_ge(s_in, 48)
                ch.step(v.tensor_copy(idxf[:, :], idx[:, :]))
                ch.step(v.tensor_tensor(onehot[:, :, :], idxf[:, :].unsqueeze(1).to_broadcast([P, E, J]),
                                        row(E).unsqueeze(2).to_broadcast([P, E, J]), ALU.is_equal))
                flat = onehot[:, :, :].rearrange("p e j -> p (e j)")
                ch.step(v.tensor_tensor_scan(cum[:, :, :].rearrange("p e j -> p (e j)"), flat, flat,
                                             0.0, ALU.add, ALU.max))
                ch.step(v.memset(small[:, 0, 0:1], 0.0))
                ch.step(v.tensor_copy(ends, cum[:, :, J - 1]))
                ch.step(v.tensor_copy(small[:, 0, 1:E], small[:, 1, 0:E - 1]))
                v.tensor_tensor(cnt[:, :], ends, prev, ALU.subtract).then_inc(s_cnt, 1)
                v.wait_ge(s_pre, 1)
                ch.step(v.tensor_scalar(nblk, ps_cnt[:, 1, :], float(P - 1), None, ALU.add))
                ch.step(v.tensor_copy(nblk_i[:, :], nblk))
                ch.step(v.tensor_scalar(nblk_i[:, :], nblk_i[:, :], 7, None, ALU.arith_shift_right))
                ch.step(v.tensor_copy(nblk, nblk_i[:, :]))
                ch.step(v.tensor_tensor_scan(last, nblk, nblk, 0.0, ALU.add, ALU.max))
                ch.step(v.tensor_tensor(first, last, nblk, ALU.subtract))
                ch.step(v.tensor_scalar(first, first, float(P), -1.0, ALU.mult, ALU.add))
                ch.step(v.tensor_tensor(first, first, prev, ALU.subtract))
                ch.step(v.tensor_tensor(off, first, ps_cnt[:, 0, :], ALU.add))
                ch.step(v.tensor_tensor(cum[:, :, :], cum[:, :, :], off.unsqueeze(2).to_broadcast([P, E, J]),
                                        ALU.add))
                ch.step(v.tensor_tensor(cum[:, :, :], cum[:, :, :], onehot[:, :, :], ALU.mult))
                ch.step(v.tensor_reduce(pos[:, :], cum[:, :, :].rearrange("p e j -> p j e"), AX.X, ALU.add))
                ch.step(v.tensor_copy(posi[:, 0, :], pos[:, :]))
                ch.step(v.tensor_scalar(posi[:, 1, :], posi[:, 0, :], 7, None, ALU.arith_shift_right))
                ch.step(v.tensor_scalar(posi[:, 0, :], posi[:, 0, :], P - 1, None, ALU.bitwise_and))
                v.tensor_copy(posf[:, :, :], posi[:, :, :]).then_inc(s_pos, 1)
                v.wait_ge(s_pos, 1)

                def chunk(q, h):
                    v.wait_ge(s_mm, q + 1)
                    v.tensor_tensor(eqp[:, h, :, :],
                                    posf[:, 0, ds(q * CH, CH)].unsqueeze(2).to_broadcast([P, CH, P]),
                                    row(P).unsqueeze(1).to_broadcast([P, CH, P]), ALU.is_equal)
                    v.tensor_tensor(eqc[:, h, :, :],
                                    posf[:, 1, ds(q * CH, CH)].unsqueeze(2).to_broadcast([P, CH, NB]),
                                    row(NB).unsqueeze(1).to_broadcast([P, CH, NB]),
                                    ALU.is_equal).then_inc(s_eq, 1)

                with v.Fori(0, NT // 4) as i:
                    chunk(i * 2, 0)
                    for k in range(4):
                        v.wait_ge(s_x[k], i * 16 + 16)
                        mom = v.bn_stats(st[:, k, 0:6], xt[:, k, :])
                    mom.then_inc(s_stat, 1)
                    v.wait_ge(s_stat, i + 1)
                    for k in range(4):
                        mom = moments(v, s_spare, st, k)
                    mom.then_inc(s_mom, 1)
                    chunk(i * 2 + 1, 1)
                    v.wait_ge(s_rstd, i * 2 + 2)
                    for k in range(4):
                        v.wait_ge(s_o[k], i * 16 + 16)
                        v.tensor_scalar(xo[:, k, :], xt[:, k, :], st[:, k, 6:7], rstd[:, 0, k:k + 1],
                                        ALU.subtract, ALU.mult).then_inc(s_ln, 1)
                v.wait_ge(s_mm, NCH + 2)
                ch.step(v.tensor_scalar(pair[:, 0, :], ps_pair[:, 1, :], float(J), -1.0, ALU.mult, ALU.add))
                ch.step(v.tensor_scalar(pair[:, 1, :], ps_pair[:, 0, :], 0.0, float(FAR), ALU.is_equal, ALU.mult))
                ch.step(v.tensor_tensor(pair[:, 0, :], pair[:, 0, :], ps_pair[:, 0, :], ALU.add))
                ch.step(v.tensor_tensor(pair[:, 0, :], pair[:, 0, :], pair[:, 1, :], ALU.add))
                ch.step(v.tensor_copy(tb["pair"][:, :], pair[:, 0, :]))
                ch.step(v.tensor_scalar(tb["tok"][:, :], tb["pair"][:, :], 2, None, ALU.arith_shift_right))
                ch.step(v.tensor_tensor(ended[:, :, :], last[0:1, :].unsqueeze(1).to_broadcast([1, NB + 2, E]),
                                        cst_r[0:1, C_ROW - C_KEEP:C_ROW - C_KEEP + NB + 2].unsqueeze(2).to_broadcast([1, NB + 2, E]),
                                        ALU.is_le))
                ch.step(v.tensor_reduce(bt[:, 0, :], ended[:, :, :], AX.X, ALU.add))
                ch.step(v.tensor_scalar(bt[:, 0, :], bt[:, 0, :], float(E - 1), None, ALU.min))
                ch.step(v.memset(bt[:, 1, 0:1], 1.0))
                ch.step(v.tensor_tensor(bt[:, 1, 1:NB + 2], bt[:, 0, 1:NB + 2], bt[:, 0, 0:NB + 1],
                                        ALU.not_equal))
                ch.step(v.tensor_tensor_scan(bt[:, 2, :], bt[:, 1, :], bt[:, 1, :], 2.0, ALU.add, ALU.max))
                ch.step(v.tensor_copy(tb["blk"][:, 2, :], bt[:, 2, :]))
                ch.step(v.tensor_scalar(tb["blk"][:, 2, :], tb["blk"][:, 2, :], 2, None, ALU.arith_shift_right))
                ch.step(v.tensor_copy(bt[:, 3, :], tb["blk"][:, 2, :]))
                ch.step(v.tensor_scalar(bt[:, 3, :], bt[:, 3, :], float(-NS), None, ALU.mult))
                ch.step(v.tensor_tensor(bt[:, 3, :], bt[:, 3, :], bt[:, 2, :], ALU.add))
                ch.step(v.tensor_scalar(bt[:, 3, :], bt[:, 3, :], float(WROW), float(SLOT0), ALU.mult, ALU.add))
                ch.step(v.tensor_tensor(bt[:, 1, :], bt[:, 1, :], bt[:, 3, :], ALU.mult))
                ch.step(v.tensor_copy(tb["blk"][:, 0:2, :], bt[:, 0:2, :]))
                ch.step(v.tensor_copy(tb["blk"][:, 2, :], bt[:, 3, :]))

            @block.scalar
            def _(a):
                with a.Fori(0, NCH // 2) as i:
                    for h in range(2):
                        q = i * 2 + h
                        a.wait_ge(s_eq, q + 1)
                        a.activation(val[:, h, :, 1, :], eqc[:, h, :, :], ACT.Identity,
                                     scale=routing(C_COL, 1)).then_inc(s_valp, 1)

            @block.gpsimd
            def _(g):
                with g.Fori(0, NCH // 2) as i:
                    for h in range(2):
                        q = i * 2 + h
                        if h:
                            g.wait_ge(s_mom, i + 1)
                            inverse_deviation(g, s_spare_g, s_rstd, i, st, rstd)
                        g.wait_ge(s_eq, q + 1)
                        g.tensor_tensor(val[:, h, :, 0, :], eqc[:, h, :, :],
                                        routing(q * CH + (C_ROW + 1), CH).unsqueeze(2).to_broadcast([P, CH, NB]),
                                        ALU.mult).then_inc(s_valc, 1)

            @block.tensor
            def _(pe):
                pe.sem_inc(s_mm, 2)
                pe.wait_ge(s_cnt, 1)
                pe.matmul(ps_cnt[:, 0, :], routing(C_TRI, P), cnt[:, :], start=True, stop=True)
                pe.matmul(ps_cnt[:, 1, :], cst[:, C_ONE:C_ONE + P], cnt[:, :], start=True,
                          stop=True).then_inc(s_pre, 1)

                def place(q, h, first, last):
                    pe.wait_ge(s_valp, q + 1)
                    pe.wait_ge(s_valc, q + 1)
                    for j in range(CH):
                        mm = pe.matmul(ps_pair[:, :, :].rearrange("p a n -> p (a n)"), eqp[:, h, j, :],
                                       val[:, h, j, :, :].rearrange("p a n -> p (a n)"),
                                       start=(first and j == 0), stop=(last and j == CH - 1),
                                       skip_group_check=True)
                    mm.then_inc(s_mm, 1)

                place(0, 0, True, False)
                place(1, 1, False, False)
                with pe.Fori(1, NCH // 2 - 1) as i:
                    for h in range(2):
                        place(i * 2 + h, h, False, False)
                place(NCH - 2, 0, False, False)
                place(NCH - 1, 1, False, True)


def moe(nc, tb, name, w_d, xn_d, y_d):
    with ExitStack() as c:
        sb = lambda n, shape, dt=F32: c.enter_context(nc.sbuf_tensor(f"{name}_{n}", shape, dt))
        ps = lambda n: c.enter_context(nc.psum_tensor(f"{name}_{n}", [P, 2, 512], F32))
        sem = lambda n: c.enter_context(nc.semaphore(f"{name}_{n}"))
        wraw = [sb(f"wraw{r}", [P, WROW]) for r in range(NS)]
        wh, wl = sb("wh", [P, SLOT0 + NS * WROW], F32R), sb("wl", [P, SLOT0 + NS * WROW], F32R)
        it, ip = sb("it", [P, 2], I32), sb("ip", [P, 2], I32)
        xg = sb("xg", [P, 2, D])
        xh, xl = sb("xh", [P, 2, DC, P], F32R), sb("xl", [P, 2, DC, P], F32R)
        sg, hm = sb("sg", [P, 2, I]), sb("hm", [P, 2, I])
        hh, hl = sb("hh", [P, 2, IC, P], F32R), sb("hl", [P, 2, IC, P], F32R)
        ob = sb("ob", [P, 2, D])
        idle = sb("idle", [1, 2 + 2 * NS])
        psx, psg, psh, pso = ps("psx"), ps("psg"), ps("psh"), ps("pso")
        s_raw = [sem(f"raw{r}") for r in range(NS)]
        s_gat = [sem(f"gat{j}") for j in range(2)]
        s_sca = [sem(f"sca{j}") for j in range(2)]
        s_wh, s_wl = [sem("wh0"), sem("wh1")], sem("wl")
        s_zero, s_it, s_ip, s_spare = sem("zero"), sem("it"), sem("ip"), sem("spare")
        s_spare_a, s_spare_v = sem("spare_a"), sem("spare_v")
        s_xt, s_xh, s_xl = sem("xt"), sem("xh"), sem("xl")
        s_gu, s_sg, s_hm = sem("gu"), sem("sg"), sem("hm")
        s_ht, s_hh, s_hl = sem("ht"), sem("hh"), sem("hl")
        s_dn, s_ob = sem("dn"), sem("ob")
        blk = tb["blk"]
        ident = tb["cst"][:, C_ID:C_ID + P]
        rounds = lambda b, j: (b - j) * 8

        TOP = SLOT0 + (NS - 1) * WROW
        HALF = WROW // 2

        def entry(eng, which, b):
            return eng.value_load(blk[0:1, which, ds(b, 1)], min_val=0, max_val=(E - 1, TOP)[which])

        def blocks(eng, turn):
            for b in range(NS):
                turn(b, b)
            with eng.Fori(1, NB // NS - 1) as i:
                for r in range(NS):
                    turn(i * NS + r, r)
            for b in range(NB - NS, NB):
                turn(b, b % NS)

        there = lambda b: not isinstance(b, int) or b < NB

        with nc.Block() as block:
            @block.sync
            def _(sp):
                def load(b, r):
                    if not below(b, NS):
                        sp.wait_ge(s_wl, b - (NS - 1))
                    new, e = entry(sp, 1, b), entry(sp, 0, b)
                    with sp.If(new > 0):
                        sp.dma_start(wraw[r][:, :], w_d[ds(e * P, P), :]).then_inc(s_raw[r], 16)
                    with sp.Else():
                        sp.sem_inc(s_raw[r], 16)
                    sp.nop()

                blocks(sp, load)

            @block.gpsimd
            def _(g):
                def gather(b, j):
                    if not below(b, 2):
                        g.wait_ge(s_xt, b - 1)
                    g.tensor_copy(it[:, j:j + 1], tb["tok"][:, ds(b, 1)]).then_inc(s_it, 1)
                    g.wait_ge(s_it, b + 1)
                    g.sem_inc(s_spare, 1)
                    g.indirect_dma_start(xg[:, j, :], None, xn_d, bass.IndirectOffsetOnAxis(it[:, j:j + 1], 0),
                                         bounds_check=tok_max, oob_is_err=False).then_inc(s_gat[j], 16)

                def scatter(b, j):
                    g.wait_ge(s_ob, b + 1)
                    g.tensor_copy(ip[:, j:j + 1], tb["pair"][:, ds(b, 1)]).then_inc(s_ip, 1)
                    g.wait_ge(s_ip, b + 1)
                    g.sem_inc(s_spare, 1)
                    g.indirect_dma_start(y_d, bass.IndirectOffsetOnAxis(ip[:, j:j + 1], 0), ob[:, j, :], None,
                                         bounds_check=pair_max, oob_is_err=False).then_inc(s_sca[j], 16)

                tok_max, pair_max = g.alloc_register(f"{name}_tok_max"), g.alloc_register(f"{name}_pair_max")
                g.reg_mov(tok_max, T - 1)
                g.reg_mov(pair_max, NP - 1)
                g.memset(idle[:, 0:1], 0.0)
                g.memset(xg[:, :, :], 0.0).then_inc(s_zero, 1)
                g.wait_ge(s_zero, 1)
                for b in range(4):
                    gather(b, b % 2)
                with g.Fori(2, NB // 2) as i:
                    for j in range(2):
                        gather(i * 2 + j, j)
                        scatter(i * 2 + (j - 4), j)
                for b in range(NB - 4, NB):
                    scatter(b, b % 2)
                for j in range(2):
                    g.wait_ge(s_sca[j], 16 * (NB // 2))

            @block.tensor
            def _(pe):
                def turn_x(b, j):
                    pe.wait_ge(s_gat[j], rounds(b, j) + 16)
                    if not below(b, 2):
                        pe.wait_ge(s_xl, b - 1)
                    for k in range(DC):
                        mm = pe.transpose(psx[:, j, k * P:(k + 1) * P], xg[:, j, k * P:(k + 1) * P], ident)
                    mm.then_inc(s_xt, 1)

                def gate_up(b, j):
                    at = pe.snap(slot[j], min_val=0, max_val=TOP)
                    pe.wait_ge(s_wl, b + 1)
                    pe.wait_ge(s_xl, b + 1)
                    if not below(b, 2):
                        pe.wait_ge(s_hm, b - 1)
                    for k in range(DC):
                        cols = ds(at + k * 2 * I, 2 * I)
                        for n, (x, w) in enumerate(((xh, wh), (xh, wl), (xl, wh))):
                            mm = pe.matmul(psg[:, j, :], x[:, j, k, :], w[:, cols],
                                           start=(k == 0 and n == 0), stop=(k == DC - 1 and n == 2))
                    mm.then_inc(s_gu, 1)

                def down(b, j):
                    at = pe.snap(slot[j], min_val=0, max_val=TOP)
                    pe.wait_ge(s_hl, b + 1)
                    if not below(b, 2):
                        pe.wait_ge(s_ob, b - 1)
                    for k in range(IC):
                        cols = ds(at + (GU + k * D), D)
                        for n, (h, w) in enumerate(((hh, wh), (hh, wl), (hl, wh))):
                            mm = pe.matmul(pso[:, j, :], h[:, j, k, :], w[:, cols],
                                           start=(k == 0 and n == 0), stop=(k == IC - 1 and n == 2))
                    mm.then_inc(s_dn, 1)

                def turn_h(b, j):
                    pe.wait_ge(s_hm, b + 1)
                    if not below(b, 2):
                        pe.wait_ge(s_hl, b - 1)
                    for k in range(IC):
                        mm = pe.transpose(psh[:, j, k * P:(k + 1) * P], hm[:, j, k * P:(k + 1) * P], ident)
                    mm.then_inc(s_ht, 1)

                slot = [pe.alloc_register(f"{name}_slot{j}") for j in range(2)]

                def find_slot(b, j):
                    pe.reg_load(slot[j], blk[0:1, 2, ds(b, 1)])

                def turn(b, r):
                    j = r % 2
                    gate_up(b, j)
                    if there(b + 1):
                        turn_x(b + 1, 1 - j)
                    if not below(b, 1):
                        down(b - 1, 1 - j)
                    if there(b + 1):
                        find_slot(b + 1, 1 - j)
                    turn_h(b, j)

                turn_x(0, 0)
                find_slot(0, 0)
                blocks(pe, turn)
                down(NB - 1, 1)

            @block.scalar
            def _(a):
                new = [a.alloc_register(f"{name}_new_a{r}") for r in range(NS)]

                def find_new(b, r):
                    a.reg_load(new[r], blk[0:1, 1, ds(b, 1)])

                def weights_high(b, r, half):
                    at = a.snap(new[r], min_val=0, max_val=TOP)
                    if half == 0:
                        a.wait_ge(s_raw[r], (b - r) * (16 // NS) + 16)
                        a.sem_inc(s_spare_a, 1)
                        if not below(b, NS):
                            a.wait_ge(s_dn, b - (NS - 1))
                            a.sem_inc(s_spare_a, 1)
                    with a.If(at > 0):
                        a.activation(wh[:, ds(at + half * HALF, HALF)], wraw[r][:, half * HALF:(half + 1) * HALF],
                                     ACT.Copy).then_inc(s_wh[half], 1)
                    with a.Else():
                        a.activation(idle[:, ds(2 + half * NS + r, 1)], idle[:, 0:1], ACT.Copy).then_inc(s_wh[half], 1)
                    a.nop()

                def rows_high(b, j):
                    a.wait_ge(s_xt, b + 1)
                    if not below(b, 2):
                        a.wait_ge(s_gu, b - 1)
                    a.activation(xh[:, j, :, :], psx[:, j, :].rearrange("p (k n) -> p k n", k=DC),
                                 ACT.Copy).then_inc(s_xh, 1)

                def silu(b, j):
                    a.wait_ge(s_gu, b + 1)
                    if not below(b, 2):
                        a.wait_ge(s_hm, b - 1)
                    a.activation(sg[:, j, :], psg[:, j, 0:I], ACT.Silu).then_inc(s_sg, 1)

                def result(b, j):
                    a.wait_ge(s_dn, b + 1)
                    if not below(b, 2):
                        a.wait_ge(s_sca[j], rounds(b, j))
                    a.activation(ob[:, j, :], pso[:, j, :], ACT.Copy).then_inc(s_ob, 1)

                def product_high(b, j):
                    a.wait_ge(s_ht, b + 1)
                    if not below(b, 2):
                        a.wait_ge(s_dn, b - 1)
                    a.activation(hh[:, j, :, :], psh[:, j, 0:I].rearrange("p (k n) -> p k n", k=IC),
                                 ACT.Copy).then_inc(s_hh, 1)

                def turn(b, r):
                    j = r % 2
                    if there(b + 3):
                        find_new(b + 3, (r + 3) % NS)
                    silu(b, j)
                    if there(b + 1):
                        rows_high(b + 1, 1 - j)
                    if not below(b, 1):
                        result(b - 1, 1 - j)
                    product_high(b, j)
                    if there(b + 3):
                        weights_high(b + 3, (r + 3) % NS, 0)
                    if there(b + 2):
                        weights_high(b + 2, (r + 2) % NS, 1)

                a.wait_ge(s_zero, 1)
                for b in range(3):
                    find_new(b, b)
                    for half in range(2 if b < 2 else 1):
                        weights_high(b, b, half)
                    if b == 0:
                        rows_high(0, 0)
                blocks(a, turn)
                result(NB - 1, 1)

            @block.vector
            def _(v):
                new = [v.alloc_register(f"{name}_new_v{r}") for r in range(NS)]

                def find_new(b, r):
                    v.reg_load(new[r], blk[0:1, 1, ds(b, 1)])

                def weights_low(b, r, half):
                    at = v.snap(new[r], min_val=0, max_val=TOP)
                    v.wait_ge(s_wh[half], b + 1)
                    v.sem_inc(s_spare_v, 1)
                    with v.If(at > 0):
                        cols = ds(at + half * HALF, HALF)
                        ins = v.tensor_tensor(wl[:, cols], wraw[r][:, half * HALF:(half + 1) * HALF],
                                              wh[:, cols].bitcast(F32), ALU.subtract)
                        if half:
                            ins.then_inc(s_wl, 1)
                    with v.Else():
                        if half:
                            v.memset(idle[:, 1:2], 0.0).then_inc(s_wl, 1)
                        else:
                            v.nop()
                    v.nop()

                def rows_low(b, j):
                    v.wait_ge(s_xh, b + 1)
                    v.tensor_tensor(xl[:, j, :, :], psx[:, j, :].rearrange("p (k n) -> p k n", k=DC),
                                    xh[:, j, :, :].bitcast(F32), ALU.subtract).then_inc(s_xl, 1)

                def product(b, j):
                    v.wait_ge(s_sg, b + 1)
                    if not below(b, 2):
                        v.wait_ge(s_ht, b - 1)
                    v.tensor_tensor(hm[:, j, :], sg[:, j, :], psg[:, j, I:2 * I], ALU.mult).then_inc(s_hm, 1)

                def product_low(b, j):
                    v.wait_ge(s_hh, b + 1)
                    v.tensor_tensor(hl[:, j, :, :], psh[:, j, 0:I].rearrange("p (k n) -> p k n", k=IC),
                                    hh[:, j, :, :].bitcast(F32), ALU.subtract).then_inc(s_hl, 1)

                def turn(b, r):
                    j = r % 2
                    if there(b + 3):
                        find_new(b + 3, (r + 3) % NS)
                    product(b, j)
                    if there(b + 1):
                        rows_low(b + 1, 1 - j)
                    product_low(b, j)
                    if there(b + 3):
                        weights_low(b + 3, (r + 3) % NS, 0)
                    if there(b + 2):
                        weights_low(b + 2, (r + 2) % NS, 1)

                for b in range(3):
                    find_new(b, b)
                    for half in range(2 if b < 2 else 1):
                        weights_low(b, b, half)
                    if b == 0:
                        rows_low(0, 0)
                blocks(v, turn)


def attend(nc, tb, d):
    NG, HG, TB = H // 4, 4, S // P
    CQ = 3 * D
    STK = 16 * (2 * HG + 2)
    SCALE = float(HD) ** -0.5
    RX = TB
    A_AT = [range(14, 16)] * 2 + [range(6, 16), range(8, 16)]
    RY, NY = 4, TB * K

    def uses(last):
        found = []
        for g in range(NG):
            if not (last and g >= 2):
                found += [("q", g), ("k", g)]
            if g == 1 and not last:
                found += [("x", t) for t in range(TB)]
            if g == 3 and not last:
                found += [("v", t) for t in range(TB)]
            if not (last and g == 3):
                found += [("m", g)]
            if g == 3:
                found += [("o", t) for t in range(TB)]
        return found

    FIRST = [("x", t) for t in range(TB)] + [("q", 0), ("k", 0), ("q", 1), ("k", 1), ("m", 0)]
    FIRST += [("v", t) for t in range(TB)]
    N0, NU = len(FIRST), len(uses(False))
    A0 = AU = TB
    D0, DU = N0 - A0, NU - AU

    class Bank:

        def __init__(self, b):
            self.b = b
            self.first = b is None
            self.order = FIRST if self.first else uses(isinstance(b, int))
            self.base = 0 if self.first else b * NU + N0

        def number(self, name, i):
            return self.base + self.order.index((name, i))

        def bank(self, name, i):
            return (self.order.index((name, i)) + (0 if self.first else N0)) % 2

        def reads(self, n):
            acts = sum(x == "v" for x, _ in self.order[:max(n, 0)])
            vecs = max(n, 0) - acts
            if self.first:
                return acts, vecs
            if n < 0:
                vecs -= 1
            return self.b * AU + (A0 + acts), self.b * DU + (D0 + vecs)

        def freed(self, name, i):
            return self.reads(self.order.index((name, i)) - 1)

        def read(self, name, i):
            return self.reads(self.order.index((name, i)) + 1)

    with ExitStack() as c:
        sb = lambda n, shape, dt=F32: c.enter_context(nc.sbuf_tensor(f"a_{n}", shape, dt))
        ps = lambda n, shape: c.enter_context(nc.psum_tensor(f"a_{n}", shape, F32))
        sem = lambda n: c.enter_context(nc.semaphore(f"a_{n}"))
        cst = tb["cst"]
        ident = cst[:, C_ID:C_ID + P]
        wqkv = [sb(f"wqkv_{n}", [P, DC, CQ], F32R) for n in "hl"]
        wout = [sb(f"wout_{n}", [P, DC, D], F32R) for n in "hl"]
        bqk = sb("bqk", [P, 2 * DC])
        wk = sb("wk", [P, NT * K])
        masks = sb("masks", [P, 3, P], BF16)
        stq, stk = sb("stq", [KROWS, 2 * HG, S], F32R), sb("stk", [KROWS, 2 * HG, S], F32R)
        qk3 = sb("qk3", [P, 2, 3, S], F32R)
        biases = sb("biases", [64 + HG * TB, 2, S], F32R)
        bias_r, brow = biases[0:H, :, :], biases[32:34, :, :]
        y4 = sb("y4", [P, RY, D])
        xt = sb("xt", [P, TB, D])
        xn = sb("xn", [P, RX, D])
        free = sb("free", [P, 1])
        xth, xtl = sb("xth", [P, DC, S], F32R), sb("xtl", [P, DC, S], F32R)
        vt = sb("vt", [P, TB, D])
        mx = sb("mx", [P, 2, HG * TB])
        small = sb("small", [34, P], F32R)
        ones2 = small[32:34, :]
        mh, ml = biases[64:64 + HG * TB, 0, 0:P], small[0:HG * TB, :]
        pt = [sb("pt0", [P, HG, S]), sb("pt1", [P, HG, S - P])]
        ct = sb("ct", [P, S])
        cth, ctl = sb("cth", [P, DC, S], F32R), sb("ctl", [P, DC, S], F32R)
        x2 = sb("x2", [P, TB, D])
        st, rstd = sb("st", [P, 2, 4, 8]), sb("rstd", [P, 2, 2, 4])
        s_spare_v, s_spare_g, s_spare_s = sem("spare_v"), sem("spare_g"), sem("spare_s")

        with ExitStack() as c1:
            bias, ones_r = xt[0:H, 0, :], qk3[0:H, 0, 0, :]
            rows, rows_l, ones = xt[32:33, 1:3, :], xth[32:33, 0:2, :], xt[32:34, 0, 0:P]
            sem1 = lambda n: c1.enter_context(nc.semaphore(f"a_{n}"))
            s_wh, s_wl, s_rows, s_in, s_c, s_bh, s_bl = (sem1(n) for n in ("wh", "wl", "rows", "in", "c", "bh", "bl"))
            s_ld = [sem1(f"ld{r}") for r in range(RY)]
            pieces = [(k, n) for n in range(4) for k in range(DC)]
            half = lambda w, k, n: wqkv[w][:, k, n * D:(n + 1) * D] if n < 3 else wout[w][:, k, :]
            with nc.Block() as block:
                @block.sync
                def _(sp):
                    for i, (k, n) in enumerate(pieces):
                        if i >= RY:
                            sp.wait_ge(s_wl, i - RY + 1)
                        sp.dma_start(y4[:, i % RY, :], d["wqkv"][:, k, n * D:(n + 1) * D] if n < 3
                                     else d["wout"][:, k, :]).then_inc(s_ld[i % RY], 16)
                    sp.wait_ge(s_c, 2)
                    for row in (0, 1):
                        for st_, at in ((stq, 3 * HD), (stk, 3 * HD + 2)):
                            sp.dma_start(raw(st_[at + row:at + row + 1, :, :]),
                                         raw(qk3[0:2 * HG, 0, 0, :])).then_inc(s_rows, 16)
                    sp.wait_ge(s_bl, 1)
                    sp.dma_start(raw(biases[33:34, :, :]), raw(rows_l)).then_inc(s_rows, 16)
                    sp.wait_ge(s_rows, 80)

                @block.scalar
                def _(a):
                    for dst, src in ((bqk[:, :], d["bqk"]), (rows, d["bvo"]), (wk[:, :], d["wk"]),
                                     (bias, d["bias"])):
                        a.dma_start(dst, src).then_inc(s_in, 16)
                    for i, (k, n) in enumerate(pieces):
                        a.wait_ge(s_ld[i % RY], 16 * (i // RY + 1))
                        a.activation(half(0, k, n), y4[:, i % RY, :], ACT.Copy,
                                     scale=1.0 if n else SCALE).then_inc(s_wh, 1)
                    a.wait_ge(s_in, 64)
                    a.activation(bqk[:, 0:DC], bqk[:, 0:DC], ACT.Copy, scale=SCALE)
                    a.activation(biases[32:33, :, :], rows, ACT.Copy).then_inc(s_bh, 1)

                @block.vector
                def _(v):
                    for i, (k, n) in enumerate(pieces):
                        v.wait_ge(s_wh, i + 1)
                        v.scalar_tensor_tensor(half(1, k, n), y4[:, i % RY, :], 1.0 if n else SCALE,
                                               half(0, k, n).bitcast(F32), ALU.mult,
                                               ALU.subtract).then_inc(s_wl, 1)
                    v.wait_ge(s_bh, 1)
                    v.tensor_tensor(rows_l, rows, biases[32:33, :, :].bitcast(F32), ALU.subtract).then_inc(s_bl, 1)

                @block.gpsimd
                def _(g):
                    g.memset(ones, 1.0)
                    g.memset(bias_r[:, 1, :].bitcast(F32), 1.0).then_inc(s_c, 1)
                    g.wait_ge(s_c, 1)
                    g.tensor_copy(ones2, ones)
                    g.tensor_copy(ones_r, bias_r[:, 1, :].bitcast(F32)).then_inc(s_c, 1)
                    g.wait_ge(s_c, 2)
                    g.wait_ge(s_in, 64)
                    g.tensor_copy(bias_r[:, 0, :], bias).then_inc(s_c, 1)
                    g.wait_ge(s_c, 3)
                    g.tensor_tensor(bias_r[:, 1, :], bias, bias_r[:, 0, :].bitcast(F32), ALU.subtract)
                    g.tensor_copy(masks[:, :, :], cst[:, C_ID:C_ID + 3 * P].rearrange("p (m n) -> p m n", m=3))
                    g.tensor_scalar(wk[:, :], wk[:, :], 0.5, None, ALU.mult)
                    g.memset(rstd[:, :, 1, :], -0.5)

        psa, psb, psw = ps("psa", [P, 2, S]), ps("psb", [P, 2, S]), ps("psw", [P, 2, S])
        psc, pss = ps("psc", [P, S]), ps("pss", [P, S])
        s_y = [sem(f"y{r}") for r in range(RY)]
        s_xin, s_acc, s_x1o = sem("xin"), sem("acc"), sem("x1o")
        s_st, s_mom, s_rd, s_xn = sem("st"), sem("mom"), sem("rd"), sem("xn")
        s_w, s_wfa, s_wfd = sem("w"), sem("wfa"), sem("wfd")
        s_xh, s_qc, s_qh, s_stk = sem("xh"), sem("qc"), sem("qh"), sem("stk")
        s_a, s_am, s_mh, s_mr = sem("a"), sem("am"), sem("mh"), sem("mr")
        s_b, s_e, s_pv = sem("b"), sem("e"), sem("pv")
        s_rs, s_ct, s_cc, s_ch = sem("rs"), sem("ct"), sem("cc"), sem("ch")
        s_xr, s_x2, s_x2o = sem("xr"), sem("x2"), sem("x2o")
        s_mom2, s_rd2, s_n2 = sem("mom2"), sem("rd2"), sem("n2")
        s_n2o = [sem(f"n2o{r}") for r in range(RX)]
        stored = lambda b, r: b * (16 * len(range(r, TB, RX)))
        whole = lambda b: isinstance(b, int)

        with nc.Block() as block:
            @block.sync
            def _(sp):
                def load_x(b):
                    if not (whole(b) and b == 0):
                        sp.wait_ge(s_xn, b * TB)
                        sp.sem_inc(s_spare_s, 1)
                        sp.wait_ge(s_x1o, b * 16)
                    sp.sem_inc(s_spare_s, 1)
                    sp.dma_start(xt[:, :, :], d["x"][ds(b * S, S), :].rearrange("(t p) n -> p t n", p=P)
                                 ).then_inc(s_xin, 16)

                def load_rows(b, some):
                    for m in some:
                        k, t, r = m // TB, m % TB, m % RY
                        if not (whole(b) and b == 0 and m < RY):
                            sp.wait_ge(s_acc, b * NY + (m - RY + 1))
                        sp.sem_inc(s_spare_s, 1)
                        sp.dma_start(y4[:, r, :], d["y"][ds((b * S + t * P) * K, P * K), :].rearrange(
                            "(p k) n -> p k n", k=K)[:, k, :]).then_inc(s_y[r], 16)

                def store_x1(b):
                    sp.wait_ge(s_acc, b * NY + NY)
                    sp.sem_inc(s_spare_s, 1)
                    sp.dma_start(d["x1"][ds(b * S, S), :].rearrange("(t p) n -> p t n", p=P), xt[:, :, :]
                                 ).then_inc(s_x1o, 16)

                def stacks(u, g4):
                    slot = (g4 % 2) * HG
                    sp.wait_ge(s_qh, u + 1)
                    if not below(u, 2):
                        sp.wait_ge(s_b, u * 16 - 16)
                    for j in range(HG):
                        rows = slice(j * HD, (j + 1) * HD)
                        for n, to in enumerate((stq, stk)):
                            sp.dma_start(raw(to[0:3 * HD, slot + j, :]), raw(qk3[rows, n, :, :])).then_inc(s_stk, 16)
                    for r in range(2):
                        sp.dma_start(raw(stk[3 * HD + r:3 * HD + r + 1, slot:slot + HG, :]),
                                     raw(bias_r[g4 * HG:(g4 + 1) * HG, r, :])).then_inc(s_stk, 16)

                def residual(b):
                    if not (whole(b) and b == 0):
                        sp.wait_ge(s_x2o, b * 16)
                        sp.sem_inc(s_spare_s, 1)
                        sp.wait_ge(s_n2, b * TB + 1)
                        sp.sem_inc(s_spare_s, 1)
                    sp.wait_ge(s_x1o, b * 16 + 16)
                    sp.sem_inc(s_spare_s, 1)
                    sp.dma_start(x2[:, :, :], d["x1"][ds(b * S, S), :].rearrange("(t p) n -> p t n", p=P)
                                 ).then_inc(s_xr, 16)

                def batch(b):
                    last = whole(b)
                    for g in range(NG):
                        if g == 0 and not last:
                            load_rows(b + 1, range(RY))
                            load_x(b + 1)
                            load_rows(b + 1, range(RY, NY // 2))
                        if g == 1 and not last:
                            load_rows(b + 1, range(NY // 2 + RY, NY))
                        if not (last and g >= 2):
                            stacks(b * NG + (g + 2), (g + 2) % NG)
                        if g == 0 and not last:
                            load_rows(b + 1, range(NY // 2, NY // 2 + RY))
                        if g == 1 and not last:
                            store_x1(b + 1)
                        if g == 1:
                            residual(b)

                load_x(0)
                load_rows(0, range(NY))
                store_x1(0)
                stacks(0, 0)
                stacks(1, 1)
                with sp.Fori(0, B - 1) as b:
                    batch(b)
                batch(B - 1)

            @block.gpsimd
            def _(g):
                def inverse(b, which, mom, rd):
                    g.wait_ge(mom, b + 1)
                    inverse_deviation(g, s_spare_g, rd, b, st[:, which, :, :], rstd[:, which, :, :])

                def split_context(b, g4):
                    u = b * NG + g4
                    g.wait_ge(s_ct, u + 1)
                    g.sem_inc(s_spare_g, 1)
                    g.wait_ge(s_w, b * NU + N0)
                    g.sem_inc(s_spare_g, 1)
                    g.tensor_copy(cth[:, g4, :], ct[:, :]).then_inc(s_cc, 1)
                    g.wait_ge(s_cc, u + 1)
                    g.tensor_tensor(ctl[:, g4, :], ct[:, :], cth[:, g4, :].bitcast(F32),
                                    ALU.subtract).then_inc(s_ch, 1)

                def outputs(b):
                    at = ds(b * S, S)
                    inverse(b, 1, s_mom2, s_rd2)
                    g.wait_ge(s_x2, b + 1)
                    g.sem_inc(s_spare_g, 1)
                    g.dma_start(d["x2"][at, :].rearrange("(t p) n -> p t n", p=P), x2[:, :, :]).then_inc(s_x2o, 16)
                    for t in range(TB):
                        g.wait_ge(s_n2, b * TB + (t + 2))
                        g.sem_inc(s_spare_g, 1)
                        g.dma_start(d["xn"][ds(b * S + t * P, P), :], xn[:, t % RX, :]).then_inc(s_n2o[t % RX], 16)

                def batch(b):
                    last = whole(b)
                    for g4 in range(NG):
                        if g4 == 1 and not last:
                            inverse(b + 1, 0, s_mom, s_rd)
                        split_context(b, g4)
                    outputs(b)

                inverse(0, 0, s_mom, s_rd)
                with g.Fori(0, B - 1) as b:
                    batch(b)
                batch(B - 1)
                g.wait_ge(s_x2o, 16 * B)
                for r in range(RX):
                    g.wait_ge(s_n2o[r], stored(B, r))

            @block.tensor
            def _(pe):
                def take(bk, name, i):
                    acts, vecs = bk.freed(name, i)
                    for s, n in ((s_wfa, acts), (s_wfd, vecs)):
                        if not (bk.first and n == 0):
                            pe.wait_ge(s, n)
                    return psw[:, bk.bank(name, i), :]

                def product(out, lhs, rhs, chunks, begun=False):
                    for k in chunks:
                        for n, (p, q) in enumerate(((0, 0), (0, 1), (1, 0))):
                            mm = pe.matmul(out, lhs[p](k), rhs[q](k), start=(k == 0 and n == 0 and not begun),
                                           stop=(k == DC - 1 and n == 2))
                    return mm

                def biased(out, which, lhs, rhs):
                    pe.matmul(out, ones2, brow[:, which, :], start=True, stop=False)
                    return product(out, lhs, rhs, range(DC), begun=True)

                def turn_x(bk, nb, t):
                    out = take(bk, "x", t)
                    pe.wait_ge(s_xn, nb * TB + (t + 1))
                    for k in range(DC):
                        mm = pe.transpose(out[:, k * P:(k + 1) * P], xn[:, t % RX, k * P:(k + 1) * P], ident)
                    mm.then_inc(s_w, 1)

                def project(out, g4, n, chunks):
                    cols = slice(n * D + g4 * P, n * D + (g4 + 1) * P)
                    return product(out, [lambda k, w=w: w[:, k, cols] for w in wqkv],
                                   [lambda k, x=x: x[:, k, :] for x in (xth, xtl)], chunks)

                def scores_row(u, slot, j, *tiles):
                    h = slot * HG + j
                    for t in tiles:
                        n = j * TB + t
                        if not (below(u, 1) and n < 2):
                            pe.wait_ge(s_am, u * 16 + (n - 1))
                        out = psa[:, t % 2, 0:(t + 1) * P]
                        pe.matmul(out, stq[0:3 * HD + 2, h, t * P:(t + 1) * P], stk[0:3 * HD + 2, h, 0:(t + 1) * P],
                                  start=True, stop=False)
                        pe.matmul(psa[:, t % 2, t * P:(t + 1) * P], masks[:, 0, :], masks[:, 1, :],
                                  start=False, stop=True).then_inc(s_a, 1)

                def turn_maxima(bk, u, i, slot):
                    out = take(bk, "m", i)
                    pe.wait_ge(s_am, u * 16 + 16)
                    pe.transpose(out[0:HG * TB, 0:P], mx[:, slot, :], ident).then_inc(s_w, 1)

                def values(bk, tiles):
                    for t in tiles:
                        out = take(bk, "v", t)
                        biased(out, 0, [lambda k, x=x: x[:, k, t * P:(t + 1) * P] for x in (xth, xtl)],
                               [lambda k, w=w: w[:, k, 2 * D:3 * D] for w in wqkv]).then_inc(s_w, 1)

                def output(bk, b):
                    pe.wait_ge(s_ch, b * NG + NG)
                    for t in range(TB):
                        out = take(bk, "o", t)
                        biased(out, 1, [lambda k, x=x: x[:, k, t * P:(t + 1) * P] for x in (cth, ctl)],
                               [lambda k, w=w: w[:, k, :] for w in wout]).then_inc(s_w, 1)

                def context(u, g, kt, part):
                    if part == 0:
                        pe.wait_ge(s_e, u * 16 + (kt * HG + HG + 1))
                        if kt == 0 and not below(u, 1):
                            pe.wait_ge(s_ct, u)
                    for j in range(HG):
                        at = (g * HG + j) * HD
                        mm = pe.matmul((psc, pss)[part][j * HD:(j + 1) * HD, kt * P:S],
                                       cst[:, C_ONE:C_ONE + HD] if part else vt[:, kt, at:at + HD],
                                       pt[kt % 2][:, j, 0:S - kt * P], start=(kt == 0), stop=(kt == TB - 1),
                                       skip_group_check=True)
                    if part == 1:
                        mm.then_inc(s_pv, 1)

                def attention(bk, b, g, qk_on, a_on):
                    u = b * NG + g
                    pe.wait_ge(s_mr, u * 32 + 32)
                    if g == 0:
                        pe.wait_ge(s_wfa, b * TB + TB)
                    for kt in range(TB):
                        for j in range(HG):
                            n, h = kt * HG + j, (g % 2) * HG + j
                            pe.wait_ge(s_e, u * 16 + n)
                            out = psb[:, n % 2, 0:S - kt * P]
                            pe.matmul(out, stk[:, h, kt * P:(kt + 1) * P], stq[:, h, kt * P:S],
                                      start=True, stop=False)
                            pe.matmul(psb[:, n % 2, 0:P], masks[:, 0, :], masks[:, 2, :],
                                      start=False, stop=True).then_inc(s_b, 1)
                            if kt == 0 and qk_on:
                                if j == 0:
                                    k_out = take(bk, "k", g)
                                mm = project(k_out, (g + 2) % NG, 1, (j,))
                                if j == HG - 1:
                                    mm.then_inc(s_w, 1)
                            if kt and j % 2:
                                context(u, g, kt - 1, j // 2)
                            if a_on and n in A_AT[g]:
                                if n == A_AT[g][0]:
                                    pe.wait_ge(s_stk, u * STK + 2 * STK)
                                i = A_AT[g].index(n)
                                scores_row(u + 1, (g + 1) % 2, i // TB, i % TB)
                    for part in (0, 1):
                        context(u, g, TB - 1, part)

                def batch(b):
                    last, bk = whole(b), Bank(b)
                    for g in range(NG):
                        u = b * NG + g
                        qk_on, a_on = not (last and g >= 2), not (last and g == 3)
                        if qk_on:
                            out = take(bk, "q", g)
                            if g == 2:
                                pe.wait_ge(s_wfd, bk.read("x", TB - 1)[1])
                            project(out, (g + 2) % NG, 0, range(DC)).then_inc(s_w, 1)
                        attention(bk, b, g, qk_on, a_on)
                        if a_on:
                            if g == 3:
                                values(bk, (0, 1))
                            for j in range(HG):
                                scores_row(u + 1, (g + 1) % 2, j,
                                           *[t for t in range(TB) if j * TB + t >= len(A_AT[g])])
                                if g == 1 and j and not last:
                                    turn_x(bk, b + 1, j - 1)
                                if g == 3 and j < 2:
                                    values(bk, (2 + j,))
                            if g == 1 and not last:
                                turn_x(bk, b + 1, TB - 1)
                            turn_maxima(bk, u + 1, g, (g + 1) % 2)
                    output(bk, b)

                bk = Bank(None)
                pe.sem_inc(s_pv, 1)
                for t in range(TB):
                    turn_x(bk, 0, t)
                pe.wait_ge(s_wfd, TB)
                for g in range(2):
                    for n, name in enumerate("qk"):
                        project(take(bk, name, g), g, n, range(DC)).then_inc(s_w, 1)
                pe.wait_ge(s_stk, STK)
                for j in range(HG):
                    scores_row(0, 0, j, *range(TB))
                turn_maxima(bk, 0, 0, 0)
                values(bk, range(TB))
                with pe.Fori(0, B - 1) as b:
                    batch(b)
                batch(B - 1)

            @block.scalar
            def _(a):
                def high(bk, u, i, g4, n):
                    name = "qk"[n]
                    a.wait_ge(s_w, bk.number(name, i) + 1)
                    if not below(u, 1):
                        a.wait_ge(s_stk, u * STK)
                    a.activation(qk3[:, n, 0:2 + n:1 + n, :],
                                 psw[:, bk.bank(name, i), :].unsqueeze(1).to_broadcast([P, 2, S]), ACT.Identity,
                                 bias=bqk[:, n * DC + g4:n * DC + g4 + 1]).then_inc(s_qc, 1)

                def rows_high(bk, b):
                    for t in range(TB):
                        a.wait_ge(s_w, bk.number("x", t) + 1)
                        a.activation(xth[:, :, t * P:(t + 1) * P],
                                     psw[:, bk.bank("x", t), :].rearrange("p (k n) -> p k n", k=DC),
                                     ACT.Copy).then_inc(s_xh, 1)

                def values(bk):
                    for t in range(TB):
                        a.wait_ge(s_w, bk.number("v", t) + 1)
                        a.activation(vt[:, t, :], psw[:, bk.bank("v", t), :], ACT.Copy).then_inc(s_wfa, 1)

                def probabilities(u, kt):
                    for j in range(HG):
                        n = kt * HG + j
                        a.wait_ge(s_b, u * 16 + (n + 1))
                        if j == 0:
                            a.wait_ge(s_pv, u * 4 + kt)
                        a.activation(pt[kt % 2][:, j, 0:S - kt * P], psb[:, n % 2, 0:S - kt * P],
                                     ACT.Exp).then_inc(s_e, 1)

                def maxima(u, slot):
                    a.wait_ge(s_mh, u * 2 + 2)
                    for r, m in enumerate((mh, ml)):
                        at = 3 * HD + 2 + r
                        a.dma_start(raw(stq[at:at + 1, slot * HG:(slot + 1) * HG, :].rearrange(
                            "a h (t q) -> a (h t) q", q=P)), raw(m)).then_inc(s_mr, 16)

                def batch(b):
                    last, bk = whole(b), Bank(b)
                    for g in range(NG):
                        u = b * NG + g
                        for kt in range(TB):
                            if kt < 2 and not (last and g >= 2):
                                high(bk, u + 2, g, (g + 2) % NG, kt)
                            probabilities(u, kt)
                        if g == 1 and not last:
                            rows_high(bk, b + 1)
                        if g == 3 and not last:
                            values(bk)
                        if not (last and g == 3):
                            maxima(u + 1, (g + 1) % 2)

                bk = Bank(None)
                a.sem_inc(s_e, 1)
                rows_high(bk, 0)
                for u in range(2):
                    for n in range(2):
                        high(bk, u, u, u, n)
                maxima(0, 0)
                values(bk)
                with a.Fori(0, B - 1) as b:
                    batch(b)
                batch(B - 1)

            @block.vector
            def _(v):
                def sums(b, some):
                    for m in some:
                        k, t, r = m // TB, m % TB, m % RY
                        if m == 0:
                            v.wait_ge(s_xin, b * 16 + 16)
                        v.wait_ge(s_y[r], b * (NY // RY * 16) + (m // RY + 1) * 16)
                        if k:
                            v.wait_ge(s_acc, b * NY + (m - TB + 1))
                        v.scalar_tensor_tensor(xt[:, t, :], y4[:, r, :], wk[:, ds(b * NY + (t * K + k), 1)],
                                               xt[:, t, :], ALU.mult, ALU.add).then_inc(s_acc, 1)

                def means(b):
                    v.wait_ge(s_acc, b * NY + NY)
                    for t in range(TB):
                        ins = v.bn_stats(st[:, 0, t, 0:6], xt[:, t, :])
                    ins.then_inc(s_st, 1)
                    v.wait_ge(s_st, b + 1)
                    for t in range(TB):
                        ins = moments(v, s_spare_v, st[:, 0, :, :], t)
                    ins.then_inc(s_mom, 1)

                def normed(out, src, which, t):
                    return v.tensor_scalar(out, src, st[:, which, t, 6:7], rstd[:, which, 0, t:t + 1],
                                           ALU.subtract, ALU.mult)

                def row(bk, b, t):
                    if t == 0:
                        v.wait_ge(s_rd, b * 2 + 2)
                    if t >= RX:
                        v.wait_ge(s_w, bk.number("x", t - RX) + 1)
                    elif not bk.first:
                        v.wait_ge(s_n2o[t], stored(b - 1, t))
                    normed(xn[:, t % RX, :], xt[:, t, :], 0, t).then_inc(s_xn, 1)

                def row_low(bk, b, t):
                    v.wait_ge(s_xh, b * TB + (t + 1))
                    at = slice(t * P, (t + 1) * P)
                    v.tensor_tensor(xtl[:, :, at], psw[:, bk.bank("x", t), :].rearrange("p (k n) -> p k n", k=DC),
                                    xth[:, :, at].bitcast(F32), ALU.subtract).then_inc(s_wfd, 1)

                def low(bk, u, i, g4, n):
                    v.wait_ge(s_qc, u * 2 + (n + 1))
                    v.scalar_tensor_tensor(qk3[:, n, 2 - n, :], psw[:, bk.bank("qk"[n], i), :],
                                           bqk[:, n * DC + g4:n * DC + g4 + 1], qk3[:, n, 0, :].bitcast(F32),
                                           ALU.add, ALU.subtract).then_inc(s_wfd, 1)
                    if n:
                        v.memset(free[:, :], 0.0).then_inc(s_qh, 1)

                def maxima(u, slot, j):
                    for t in range(TB):
                        n = j * TB + t
                        v.wait_ge(s_a, u * 16 + (n + 1))
                        v.tensor_reduce(mx[:, slot, n:n + 1], psa[:, t % 2, 0:(t + 1) * P], AX.X,
                                        ALU.max).then_inc(s_am, 1)

                def negated(bk, u, i):
                    src = psw[0:HG * TB, bk.bank("m", i), 0:P]
                    v.wait_ge(s_w, bk.number("m", i) + 1)
                    if not below(u, 1):
                        v.wait_ge(s_mr, u * 32)
                    v.tensor_scalar(mh, src, -1.0, None, ALU.mult).then_inc(s_mh, 1)
                    v.wait_ge(s_mh, u * 2 + 1)
                    v.scalar_tensor_tensor(ml, src, -1.0, mh.bitcast(F32), ALU.mult,
                                           ALU.subtract).then_inc(s_mh, 1)
                    v.wait_ge(s_mh, u * 2 + 2)
                    v.memset(free[:, :], 0.0).then_inc(s_wfd, 1)

                def normalise(u):
                    v.wait_ge(s_pv, u * 4 + 5)
                    if not below(u, 1):
                        v.wait_ge(s_ch, u)
                    v.reciprocal(ct[:, :], pss[:, :]).then_inc(s_rs, 1)
                    v.wait_ge(s_rs, u + 1)
                    v.tensor_tensor(ct[:, :], psc[:, :], ct[:, :], ALU.mult).then_inc(s_ct, 1)

                def output(bk, b):
                    v.wait_ge(s_xr, b * 16 + 16)
                    for t in range(TB + 1):
                        if t < TB:
                            v.wait_ge(s_w, bk.number("o", t) + 1)
                            v.tensor_tensor(x2[:, t, :], psw[:, bk.bank("o", t), :], x2[:, t, :],
                                            ALU.add).then_inc(s_wfd, 1)
                        if t:
                            v.wait_ge(s_wfd, bk.read("o", t - 1)[1])
                            ins = v.bn_stats(st[:, 1, t - 1, 0:6], x2[:, t - 1, :])
                    ins.then_inc(s_x2, 1)
                    v.wait_ge(s_x2, b + 1)
                    for t in range(TB):
                        ins = moments(v, s_spare_v, st[:, 1, :, :], t)
                    ins.then_inc(s_mom2, 1)
                    v.wait_ge(s_rd2, b * 2 + 2)
                    for t in range(TB):
                        if t >= RX:
                            v.wait_ge(s_n2o[t % RX], stored(b, t % RX) + 16)
                        elif whole(b):
                            v.wait_ge(s_n2o[t], stored(b, t))
                        normed(xn[:, t % RX, :], x2[:, t, :], 1, t).then_inc(s_n2, 1)

                def batch(b):
                    last, bk = whole(b), Bank(b)
                    for g in range(NG):
                        u = b * NG + g
                        if not (last and g >= 2):
                            low(bk, u + 2, g, (g + 2) % NG, 0)
                        if g < 2 and not last:
                            sums(b + 1, range(g * NY // 2, (g + 1) * NY // 2))
                        if not (last and g >= 2):
                            low(bk, u + 2, g, (g + 2) % NG, 1)
                        if g == 1 and not last:
                            means(b + 1)
                        if last and g == 3:
                            normalise(u)
                        else:
                            for j in range(HG):
                                if g == 3 and j == len(A_AT[g]) // TB:
                                    normalise(u)
                                maxima(u + 1, (g + 1) % 2, j)
                                if g == 1 and not last:
                                    if j >= 2:
                                        row_low(bk, b + 1, j - 2)
                                    row(bk, b + 1, j)
                            if g == 1 and not last:
                                for t in (2, 3):
                                    row_low(bk, b + 1, t)
                            negated(bk, u + 1, g)
                        if g < 3:
                            normalise(u)
                    output(bk, b)

                bk = Bank(None)
                v.sem_inc(s_n2, 1)
                sums(0, range(NY))
                means(0)
                for t in range(TB + 2):
                    if t >= 2:
                        row_low(bk, 0, t - 2)
                    if t < TB:
                        row(bk, 0, t)
                for u in range(2):
                    for n in range(2):
                        low(bk, u, u, u, n)
                for j in range(HG):
                    maxima(0, 0, j)
                negated(bk, 0, 0)
                with v.Fori(0, B - 1) as b:
                    batch(b)
                batch(B - 1)


def final(nc, tb, d, out_d):
    with ExitStack() as c:
        sb = lambda n, shape, dt=F32: c.enter_context(nc.sbuf_tensor(f"z_{n}", shape, dt))
        sem = lambda n: c.enter_context(nc.semaphore(f"z_{n}"))
        R = 8
        y4, xt = sb("y4", [P, R, K, D]), sb("xt", [P, R, D])
        wk = sb("wk", [P, NT * K])
        s_w, s_w2 = sem("w"), sem("w2")
        s_in = [sem(f"in{r}") for r in range(R)]
        s_out = [sem(f"out{r}") for r in range(R)]
        s_done = [sem("done_v"), sem("done_g")]
        s_acc_v, s_acc_g, s_scaled, s_spare_s = sem("acc_v"), sem("acc_g"), sem("scaled"), sem("spare_s")
        with nc.Block() as block:
            @block.sync
            def _(sp):
                sp.dma_start(wk[:, :], d["wk"]).then_inc(s_w, 16)

                def load(i, r):
                    t = i * R + r
                    sp.dma_start(y4[:, r, :, :], d["y"][ds(t * (P * K), P * K), :].rearrange(
                        "(p k) n -> p k n", k=K)).then_inc(s_in[r], 16)
                    sp.dma_start(xt[:, r, :], d["x2"][ds(t * P, P), :]).then_inc(s_in[r], 16)

                def store(i, r):
                    sp.wait_ge(s_done[r % 2], i * (R // 2) + (r // 2 + 1))
                    sp.sem_inc(s_spare_s, 1)
                    sp.dma_start(out_d[ds((i * R + r) * P, P), :], xt[:, r, :]).then_inc(s_out[r], 16)

                def turn(i, last):
                    for r in range(R):
                        store(i, r)
                        r2, i2 = (r + R // 2) % R, i + r // (R // 2)
                        if not (last and r >= R // 2):
                            sp.wait_ge(s_out[r2], i2 * 16 + 16)
                            sp.sem_inc(s_spare_s, 1)
                            load(i2, r2)

                for r in range(R):
                    sp.sem_inc(s_out[r], 16)
                for r in range(R // 2):
                    load(0, r)
                with sp.Fori(0, NT // R - 1) as i:
                    turn(i, False)
                turn(NT // R - 1, True)
                for r in range(R):
                    sp.wait_ge(s_out[r], NT // R * 16 + 16)

            @block.vector
            def _(v):
                v.wait_ge(s_w, 16)
                v.tensor_scalar(wk[:, :], wk[:, :], 0.5, None, ALU.mult).then_inc(s_w2, 1)
                v.wait_ge(s_w2, 1)
                with v.Fori(0, NT // R) as i:
                    for m, r in enumerate(range(0, R, 2)):
                        t, at = i * R + r, i * (R // 2 * (K - 1)) + m * (K - 1)
                        v.wait_ge(s_in[r], i * 32 + 32)
                        for k in range(K):
                            if k:
                                v.wait_ge(s_acc_v, at + k)
                            v.scalar_tensor_tensor(xt[:, r, :], y4[:, r, k, :], wk[:, ds(t * K + k, 1)],
                                                   xt[:, r, :], ALU.mult, ALU.add).then_inc(
                                                       s_acc_v if k < K - 1 else s_done[0], 1)

            @block.scalar
            def _(a):
                a.wait_ge(s_w2, 1)
                with a.Fori(0, NT // R) as i:
                    for r in range(1, R, 2):
                        t = i * R + r
                        a.wait_ge(s_in[r], i * 32 + 32)
                        for k in range(K):
                            ins = a.activation(y4[:, r, k, :], y4[:, r, k, :], ACT.Copy,
                                               scale=wk[:, ds(t * K + k, 1)])
                        ins.then_inc(s_scaled, 1)

            @block.gpsimd
            def _(g):
                with g.Fori(0, NT // R) as i:
                    for m, r in enumerate(range(1, R, 2)):
                        at = i * (R // 2 * (K - 1)) + m * (K - 1)
                        g.wait_ge(s_scaled, i * (R // 2) + (m + 1))
                        for k in range(K):
                            if k:
                                g.wait_ge(s_acc_g, at + k)
                            g.tensor_tensor(xt[:, r, :], xt[:, r, :], y4[:, r, k, :], ALU.add).then_inc(
                                s_acc_g if k < K - 1 else s_done[1], 1)


def macaron(nc, x, idx, wk, w, wqkv, bqk, bvo, wout, const, bias, out):
    with ExitStack() as c:
        sb = lambda n, shape, dt=F32: c.enter_context(nc.sbuf_tensor(n, shape, dt))
        tb = {"cst": sb("cst", [P, C_KEEP]),
              "pair": sb("pair", [P, NB], I32),
              "tok": sb("tok", [P, NB], I32),
              "blk": sb("blk", [1, 3, NB + 2], I32)}
        hbm = lambda n, shape: nc.dram_tensor(n, shape, F32, kind="Internal").ap()
        xn = hbm("xn_rows", (T, D))
        y = hbm("y_rows", (NP, D))
        d = {"x": x, "y": y, "wk": wk, "wqkv": wqkv, "bqk": bqk, "bvo": bvo, "wout": wout,
             "bias": bias, "x1": hbm("x1_rows", (T, D)), "x2": hbm("x2_rows", (T, D)), "xn": xn}
        route(nc, tb, const, idx, x, xn)
        moe(nc, tb, "f1", w, xn, y)
        attend(nc, tb, d)
        moe(nc, tb, "f2", w, xn, y)
        final(nc, tb, d, out)




def constants():
    import numpy as np
    c, r = np.zeros((P, C_END), np.float32), np.arange(P)
    c[:, C_ID:C_ID + P] = np.eye(P)
    c[:, C_MQ:C_MQ + P] = np.where(r[None, :] > r[:, None], NEG, 0.0)
    c[:, C_MK:C_MK + P] = np.where(r[:, None] > r[None, :], NEG, 0.0)
    c[:, C_TRI:C_TRI + P] = r[:, None] < r[None, :]
    c[:, C_ROW:C_ROW + 256] = np.arange(256)
    c[:, C_COL] = r
    c[:, C_ONE:C_ONE + P] = 1.0
    return c


def alibi():
    import numpy as np
    m = np.arange(1, H + 1, dtype=np.float32) * np.float32(8.0 / H)
    slopes = (np.float32(1.0) / np.float32(2.0) ** m).astype(np.float32)
    return (np.arange(1 - S, 1, dtype=np.float32)[None, :] * slopes[:, None]).astype(np.float32)


def kernel(L0_attn_x, L0_attn_Wqkv, L0_attn_b_qkv, L0_attn_Wout, L0_attn_b_out, L0_ffn_gate_weight,
           L0_ffn_up_weight, L0_ffn_down_weight, L0_ffn_topk_idx, L0_ffn_topk_weight):
    import numpy as np
    import concourse.bacc as bacc
    from concourse.bass_utils import run_bass_kernel_spmd

    put = lambda a: np.ascontiguousarray(a)
    turned = lambda a, n: np.asarray(a).transpose(0, 2, 1).reshape(E, n, P, -1)
    gu = np.concatenate([turned(L0_ffn_gate_weight, DC), turned(L0_ffn_up_weight, DC)], -1)
    gu = gu.transpose(0, 2, 1, 3).reshape(E, P, GU)
    dn = turned(L0_ffn_down_weight, IC).transpose(0, 2, 1, 3).reshape(E, P, IC * D)
    chunked = lambda a: np.asarray(a).T.reshape(DC, P, -1).transpose(1, 0, 2)
    b_qkv = np.asarray(L0_attn_b_qkv)
    arrays = {
        "x_in": put(np.asarray(L0_attn_x).reshape(T, D)),
        "idx_in": put(np.asarray(L0_ffn_topk_idx).reshape(P, J)),
        "wk_in": put(np.asarray(L0_ffn_topk_weight).reshape(NT, P, K).transpose(1, 0, 2).reshape(P, NT * K)),
        "w_in": put(np.concatenate([gu, dn], -1).reshape(E * P, WROW)),
        "wqkv_in": put(chunked(L0_attn_Wqkv)),
        "bqk_in": put(b_qkv[:2 * D].reshape(2 * DC, P).T),
        "bvo_in": put(np.stack([b_qkv[2 * D:], np.asarray(L0_attn_b_out)])[None]),
        "wout_in": put(chunked(L0_attn_Wout)),
        "const_in": constants(),
        "bias_in": alibi(),
    }
    nc = bacc.Bacc("TRN2", target_bir_lowering=False, num_devices=1)
    args = [nc.dram_tensor(n, a.shape, mybir.dt.from_np(a.dtype), kind="ExternalInput").ap()
            for n, a in arrays.items()]
    out = nc.dram_tensor("out", (T, D), F32, kind="ExternalOutput").ap()
    macaron(nc, *args, out)
    r = run_bass_kernel_spmd(nc, [arrays], core_ids=[0])
    return r.results[0]["out"].reshape(B, S, D)
```
